# Optimizing a Trainium2 kernel written in Bass

```python
import numpy as np
import jax
import jax.numpy as jnp

def _softmax(x, axis=-1):
    return jax.nn.softmax(x, axis=axis)

def _gelu(x):
    return jax.nn.gelu(x, approximate=True)

def _silu(x):
    return jax.nn.silu(x)

def _sigmoid(x):
    return jax.nn.sigmoid(x)

def _layernorm(x, axis=-1, eps=1e-05):
    m = jnp.mean(x, axis=axis, keepdims=True)
    v = jnp.var(x, axis=axis, keepdims=True)
    return (x - m) / jnp.sqrt(v + eps)

def _scatter_add(tgt, idx, src, axis=0):
    return tgt.at[idx].add(src)

def _segment_sum(src, seg, n):
    return jax.ops.segment_sum(src, seg, n)
kernel_name = 'mk_gps_d1_gnn_r8_a491df'

def setup_inputs(seed: int=0):
    np.random.seed(seed)
    _w = jnp.asarray

    def _rec_inputs():
        import jax
        import jax.numpy as jnp
        _gk = jax.random.key(seed)
        x = -0.0003713 + 1 * jax.random.normal(jax.random.fold_in(_gk, 1), (6250, 256), jnp.float32)
        src = jax.random.randint(jax.random.fold_in(_gk, 2), (100000,), 0, 6250, jnp.int32)
        dst = jnp.minimum((6250 * jax.random.uniform(jax.random.fold_in(_gk, 3), (100000,)) ** 2.0).astype(jnp.int32), 49999)
        _o = jnp.argsort(dst, stable=True)
        src = src[_o]
        dst = dst[_o]
        return (x, src, dst)
    x, src, dst = _rec_inputs()

    def _L0_gnn_setup():
        import jax, jax.numpy as jnp
        import numpy as np
        N_NODES = 6250
        EPS = 1e-12
        key = jax.random.key(seed)
        k1, k2, k3 = jax.random.split(key, 3)
        d_in, d_out, n_edges = (256, 256, 100000)
        input_matrix = jax.random.normal(k1, (N_NODES, d_in), dtype=jnp.float32)
        adjacency_coo_matrix = jax.random.randint(k2, (2, n_edges), 0, N_NODES, dtype=jnp.int64)
        W = jax.random.normal(k3, (2 * d_in, d_out), dtype=jnp.float32) * (1.0 / np.sqrt(2 * d_in))
        b = jnp.zeros((d_out,), dtype=jnp.float32)
        return {'input_matrix': input_matrix, 'adjacency_coo_matrix': adjacency_coo_matrix, 'W': W, 'b': b}
    _L0_gnn_all = _L0_gnn_setup()
    _L0_gnn_in = {k: v for k, v in _L0_gnn_all.items() if k in ('W', 'b')}
    del _L0_gnn_all

    def _L0_mix_setup():
        import jax, jax.numpy as jnp
        import numpy as np
        DIM = 256
        HEADS = 4
        DIM_HEAD = 32
        NUM_MEM = 4
        HIDDEN = HEADS * DIM_HEAD
        SCALE = DIM_HEAD ** (-0.5)

        def rmsnorm(x, g):
            n = jnp.linalg.norm(x, axis=-1, keepdims=True)
            return x / jnp.maximum(n, 1e-12) * g * x.shape[-1] ** 0.5
        key = jax.random.key(seed)
        ks = jax.random.split(key, 8)
        B, N = (4, 2048)
        return {'x': jax.random.normal(ks[0], (B, N, DIM), jnp.float32), 't': jax.random.normal(ks[1], (B,), jnp.float32), 'w_qkv': jax.random.normal(ks[2], (DIM, 3 * HIDDEN), jnp.float32) * 0.02, 'mem_kv': jax.random.normal(ks[3], (2, HEADS, DIM_HEAD, NUM_MEM), jnp.float32), 'w_out': jax.random.normal(ks[4], (HIDDEN, DIM), jnp.float32) * 0.02, 'b_out': jnp.zeros((DIM,), jnp.float32), 'g_out': jnp.ones((DIM,), jnp.float32), 'g_pre': jnp.ones((DIM,), jnp.float32)}
    _L0_mix_all = _L0_mix_setup()
    _L0_mix_in = {k: v for k, v in _L0_mix_all.items() if k in ('t', 'w_qkv', 'mem_kv', 'w_out', 'b_out', 'g_out', 'g_pre')}
    del _L0_mix_all

    def _L0_ffn_setup():
        import jax, jax.numpy as jnp
        import numpy as np
        TOP_K = 2
        LN_EPS = 1e-05
        key = jax.random.key(seed)
        ks = jax.random.split(key, 8)
        B, S, D, E, H = (16, 1024, 256, 8, 1024)
        x = jax.random.normal(ks[0], (B, S, D), dtype=jnp.float32)
        Wr = jax.random.normal(ks[1], (D, E), dtype=jnp.float32) * 0.1
        br = jnp.zeros((E,), dtype=jnp.float32)
        ln_g = jnp.ones((E, D), dtype=jnp.float32)
        ln_b = jnp.zeros((E, D), dtype=jnp.float32)
        W1 = jax.random.normal(ks[2], (E, D, H), dtype=jnp.float32) * (1.0 / np.sqrt(D))
        b1 = jnp.zeros((E, H), dtype=jnp.float32)
        W2 = jax.random.normal(ks[3], (E, H, D), dtype=jnp.float32) * (1.0 / np.sqrt(H))
        b2 = jnp.zeros((E, D), dtype=jnp.float32)
        return {'x': x, 'Wr': Wr, 'br': br, 'ln_g': ln_g, 'ln_b': ln_b, 'W1': W1, 'b1': b1, 'W2': W2, 'b2': b2}
    _L0_ffn_all = _L0_ffn_setup()
    _L0_ffn_in = {k: v for k, v in _L0_ffn_all.items() if k in ('Wr', 'br', 'ln_g', 'ln_b', 'W1', 'b1', 'W2', 'b2')}
    del _L0_ffn_all
    return {'x': x, 'src': src, 'dst': dst, 'L0_gnn_W': _L0_gnn_in['W'], 'L0_gnn_b': _L0_gnn_in['b'], 'L0_mix_t': _L0_mix_in['t'], 'L0_mix_w_qkv': _L0_mix_in['w_qkv'], 'L0_mix_mem_kv': _L0_mix_in['mem_kv'], 'L0_mix_w_out': _L0_mix_in['w_out'], 'L0_mix_b_out': _L0_mix_in['b_out'], 'L0_mix_g_out': _L0_mix_in['g_out'], 'L0_mix_g_pre': _L0_mix_in['g_pre'], 'L0_ffn_Wr': _L0_ffn_in['Wr'], 'L0_ffn_br': _L0_ffn_in['br'], 'L0_ffn_ln_g': _L0_ffn_in['ln_g'], 'L0_ffn_ln_b': _L0_ffn_in['ln_b'], 'L0_ffn_W1': _L0_ffn_in['W1'], 'L0_ffn_b1': _L0_ffn_in['b1'], 'L0_ffn_W2': _L0_ffn_in['W2'], 'L0_ffn_b2': _L0_ffn_in['b2']}

def reference(x, src, dst, L0_gnn_W, L0_gnn_b, L0_mix_t, L0_mix_w_qkv, L0_mix_mem_kv, L0_mix_w_out, L0_mix_b_out, L0_mix_g_out, L0_mix_g_pre, L0_ffn_Wr, L0_ffn_br, L0_ffn_ln_g, L0_ffn_ln_b, L0_ffn_W1, L0_ffn_b1, L0_ffn_W2, L0_ffn_b2):
    import jax
    import jax.numpy as jnp

    def _L0_gnn_ref(input_matrix, adjacency_coo_matrix, W, b):
        import jax, jax.numpy as jnp
        import numpy as np
        N_NODES = 6250
        EPS = 1e-12
        src = adjacency_coo_matrix[0]
        dst = adjacency_coo_matrix[1]
        neigh_sum = jax.ops.segment_sum(input_matrix[src], dst, num_segments=N_NODES)
        deg = jax.ops.segment_sum(jnp.ones_like(dst, dtype=input_matrix.dtype), dst, num_segments=N_NODES)
        neigh_mean = neigh_sum / jnp.maximum(deg, 1.0)[:, None]
        h = jnp.concatenate([input_matrix, neigh_mean], axis=-1)
        out = jax.nn.relu(h @ W + b)
        norm = jnp.maximum(jnp.linalg.norm(out, axis=-1, keepdims=True), EPS)
        return out / norm

    def _L0_mix_ref(x, t, w_qkv, mem_kv, w_out, b_out, g_out, g_pre):
        import jax, jax.numpy as jnp
        import numpy as np
        DIM = 256
        HEADS = 4
        DIM_HEAD = 32
        NUM_MEM = 4
        HIDDEN = HEADS * DIM_HEAD
        SCALE = DIM_HEAD ** (-0.5)

        def rmsnorm(x, g):
            n = jnp.linalg.norm(x, axis=-1, keepdims=True)
            return x / jnp.maximum(n, 1e-12) * g * x.shape[-1] ** 0.5
        b, n, c = x.shape
        xn = rmsnorm(x, g_pre)
        qkv = xn @ w_qkv
        q, k, v = jnp.split(qkv, 3, axis=-1)

        def to_heads(z):
            return z.reshape(b, n, HEADS, DIM_HEAD).transpose(0, 2, 3, 1)
        q, k, v = map(to_heads, (q, k, v))
        mk = jnp.broadcast_to(mem_kv[0], (b, HEADS, DIM_HEAD, NUM_MEM))
        mv = jnp.broadcast_to(mem_kv[1], (b, HEADS, DIM_HEAD, NUM_MEM))
        k = jnp.concatenate([mk, k], axis=-1)
        v = jnp.concatenate([mv, v], axis=-1)
        q = jax.nn.softmax(q, axis=-2) * SCALE
        k = jax.nn.softmax(k, axis=-1)
        context = jnp.einsum('bhdn,bhen->bhde', k, v)
        out = jnp.einsum('bhde,bhdn->bhen', context, q)
        out = out.transpose(0, 3, 1, 2).reshape(b, n, HIDDEN)
        out = rmsnorm(out @ w_out + b_out, g_out)
        return out + x

    def _L0_ffn_ref(x, Wr, br, ln_g, ln_b, W1, b1, W2, b2):
        import jax, jax.numpy as jnp
        import numpy as np
        TOP_K = 2
        LN_EPS = 1e-05
        B, S, D = x.shape
        N = B * S
        xt = x.reshape(N, D)
        logits = xt @ Wr + br
        probs = jax.nn.softmax(logits, axis=-1)
        top_p, top_idx = jax.lax.top_k(probs, TOP_K)
        weights = top_p / top_p.sum(axis=-1, keepdims=True)
        mu = xt.mean(axis=-1, keepdims=True)
        var = ((xt - mu) ** 2).mean(axis=-1, keepdims=True)
        xn = (xt - mu) * jax.lax.rsqrt(var + LN_EPS)
        xe = xn[None, :, :] * ln_g[:, None, :] + ln_b[:, None, :]
        h = jax.nn.gelu(jnp.einsum('end,edh->enh', xe, W1) + b1[:, None, :], approximate=False)
        y = jnp.einsum('enh,ehd->end', h, W2) + b2[:, None, :]
        y_tok = jnp.transpose(y, (1, 0, 2))
        sel = jnp.take_along_axis(y_tok, top_idx[:, :, None], axis=1)
        out = (weights[:, :, None] * sel).sum(axis=1)
        return out.reshape(B, S, D)
    edge_index = jnp.stack([src, dst])
    xn = _layernorm(x, axis=-1)
    x = x + _L0_gnn_ref(xn, edge_index, L0_gnn_W, L0_gnn_b) + _L0_mix_ref(xn[None], L0_mix_t, L0_mix_w_qkv, L0_mix_mem_kv, L0_mix_w_out, L0_mix_b_out, L0_mix_g_out, L0_mix_g_pre)[0]
    x = x + _L0_ffn_ref(_layernorm(x, axis=-1)[None], L0_ffn_Wr, L0_ffn_br, L0_ffn_ln_g, L0_ffn_ln_b, L0_ffn_W1, L0_ffn_b1, L0_ffn_W2, L0_ffn_b2)[0]
    return x

_drawn_inputs = setup_inputs


def setup_inputs(seed=0):
    import zlib

    import numpy as np

    out = dict(_drawn_inputs(seed))
    spreads = {'L0_gnn_b': (0.0, 0.8),
     'L0_mix_b_out': (0.0, 0.1),
     'L0_mix_g_out': (1.0, 0.2),
     'L0_mix_g_pre': (1.0, 0.6),
     'L0_ffn_br': (0.0, 0.1),
     'L0_ffn_ln_g': (1.0, 0.2),
     'L0_ffn_ln_b': (0.0, 0.344),
     'L0_ffn_b1': (0.0, 0.328),
     'L0_ffn_b2': (0.0, 0.1)}
    factors = {'L0_mix_w_qkv': 8.0, 'L0_mix_mem_kv': 8.0, 'L0_mix_w_out': 8.0}
    for name, (base, spread) in spreads.items():
        noise = np.random.default_rng([zlib.crc32(name.encode()), seed]).standard_normal(out[name].shape)
        drawn = base * np.exp(spread * noise) if base else spread * noise
        out[name] = jnp.asarray(drawn.astype(out[name].dtype))
    for name, factor in factors.items():
        out[name] = (out[name] * factor).astype(out[name].dtype)
    return out
```

```python
from contextlib import ExitStack

import concourse.bass as bass
from concourse import mybir

F32 = mybir.dt.float32
BF16 = mybir.dt.bfloat16
I32 = mybir.dt.int32
U32 = mybir.dt.uint32
ALU = mybir.AluOpType
ACT = mybir.ActivationFunctionType
AX = mybir.AxisListType.X
ds = bass.ds

P = 128
N = 6250
D = 256
DC = D // P
NT = (N + P - 1) // P
TAIL = N - (NT - 1) * P
EDGES = 100000
EROWS = 784
EFULL, EREST = EDGES // P, EDGES % P
EJ, EP = 7, EROWS // 7
NOWHERE = 1 << 20
STEPS_J = 7
STEP_BLOCK = 8
PAIRS = STEP_BLOCK // 2
S_GROUP = 4
TILE_BITS = 6
BLOCKS = (EFULL + 1 + (NT - 1) + NT + STEP_BLOCK - 1) // STEP_BLOCK
ACCW = D + 2
HEADS, HD = 4, 32
HID = HEADS * HD
MEM = 4
KVW = 2 * HID + 2
EXPERTS, HIDDEN = 8, 1024
HC = HIDDEN // P
CAP = NT * P + P
PADROW = EXPERTS * CAP
PAYW = 266
W_AT, ID_AT = D, D + EXPERTS
MOE_TILES = 106
OUT_ROWS = NT * P + P
EPS_LN = 1e-5
TINY = 1e-12
SCALE = HD ** -0.5


class Links:

    def __init__(self, eng, sem):
        self.eng, self.sem, self.count = eng, sem, 0

    def after(self, ins):
        self.count = self.count + 1
        ins.then_inc(self.sem, 1)
        self.eng.wait_ge(self.sem, self.count)


def until(eng, sem, value):
    if isinstance(value, int) and value <= 0:
        return
    eng.wait_ge(sem, value)


def stand_alone(eng, passed):
    eng.sem_inc(passed, 1)


def repeat(eng, links, body, first, end):
    start = links.count if links else 0
    body(first)
    if end - first <= 1:
        return
    per = (links.count - start) if links else 0
    with eng.Fori(first + 1, end) as i:
        if links:
            links.count = start + (i - first) * per if per else start
        body(i)
    if links:
        links.count = start + (end - first) * per


def build_program(nc, x, src, dst, gnn_W, gnn_b, w_qkv, mem_kv, w_out, b_out, g_out, g_pre,
                  Wr, br, ln_g, ln_b, W1, b1, W2, b2, out):
    ctx = ExitStack()
    with ctx:
        def sb(name, shape, dt=F32):
            return ctx.enter_context(nc.sbuf_tensor(name, shape, dt))

        def sem(name):
            return ctx.enter_context(nc.semaphore(name))

        def dram(name, shape, dt=F32):
            return nc.dram_tensor(name, shape, dt, kind="Internal").ap()

        edges_d = dram("edges_d", (EROWS, 2, P), I32)
        z_d = dram("z_d", (NT * P, D))
        xnT_d = dram("xnT_d", (NT, P, D))
        s_d = dram("s_d", (NT, P, D))
        bu_d = dram("bu_d", (NT, P, 2 * D))
        step_d = dram("step_d", (P * STEPS_J,))
        bucket_d = dram("bucket_d", (PADROW + P, PAYW))
        moetab_d = dram("moetab_d", (2, P), I32)

        w1s = sb("w1s", [P, EXPERTS * DC * HIDDEN])
        w2s = sb("w2s", [P, EXPERTS * HC * D])
        taken = {"a": 0, "b": 0, "c": 0}
        LATE = EXPERTS * HC * D // 2

        def lend(stage, n):
            at = taken[stage]
            taken[stage] += n
            if stage != "a":
                assert at + n <= EXPERTS * HC * D - LATE
                return w2s[:, LATE + at:LATE + at + n]
            if at + n <= LATE:
                return w2s[:, at:at + n]
            at = max(at, LATE)
            taken[stage] = at + n
            at += NT * KVW - LATE
            assert at + n <= EXPERTS * DC * HIDDEN
            return w1s[:, at:at + n]

        x_all = w1s[:, 0:NT * D].rearrange("p (t d) -> p t d", d=D)
        kv_all = w1s[:, 0:NT * KVW].rearrange("p (t w) -> p t w", w=KVW)
        xn_flat = lend("a", 6 * D)
        xn = [xn_flat[:, 3 * D * h:3 * D * (h + 1)].rearrange("p (t d) -> p t d", d=D) for h in range(2)]
        xnT = [lend("a", 3 * D).rearrange("p (t d) -> p t d", d=D) for _ in range(2)]
        zs_flat = lend("a", 6 * D)
        zs = [zs_flat[:, 3 * D * h:3 * D * (h + 1)].rearrange("p (t d) -> p t d", d=D) for h in range(2)]
        ss = [lend("a", 3 * D).rearrange("p (t d) -> p t d", d=D) for _ in range(2)]
        w_neigh = lend("a", DC * D).rearrange("p (c d) -> p c d", c=DC)
        w_kv = lend("a", DC * 2 * HID).rearrange("p (c d) -> p c d", c=DC)
        headmask = lend("a", HID)
        w_outs = lend("a", D)
        mkT = lend("a", HID)[0:MEM]
        mv1 = lend("a", HID + 2)[0:MEM]
        thrL, thrF, Fr, cr, delta, junk49, pairs = (lend("a", NT) for _ in range(7))
        pairs = pairs.bitcast(I32)
        Lr = lend("a", NT + 1)
        firstlast = lend("a", 2 * EJ)
        ed_flat = lend("a", EJ * 2 * P)
        ed = ed_flat.bitcast(I32).rearrange("p (j k e) -> p j k e", j=EJ, k=2)
        steps_flat = lend("a", STEPS_J * 2 * P)
        steps_e = steps_flat.bitcast(I32).rearrange("p (j k e) -> p j k e", j=STEPS_J, k=2)
        epad = steps_flat[0:1, 0:2 * D].bitcast(I32)
        steps_f = ed_flat.rearrange("p (j k e) -> p j k e", j=STEPS_J, k=2)
        ek = zs_flat[:, 0:8 * HID].rearrange("p (t d) -> p t d", t=8)
        kmax, kmaxb, kmaxrow, ctxs, ctxT = (xn_flat[:, k * HID:(k + 1) * HID] for k in range(5))

        acc = sb("acc", [P, NT + 1, ACCW])
        acc_flat = acc[:, :, :].rearrange("p t w -> p (t w)")
        srcT = sb("srcT", [P, P * STEPS_J], I32)
        dstT = sb("dstT", [P, P * STEPS_J])
        G = sb("G", [P, STEP_BLOCK, ACCW])
        S = sb("S", [P, 2, S_GROUP, P])
        ident = sb("ident", [P, P])
        iota = sb("iota", [P, P])
        before = sb("before", [P, P], BF16)
        ones_b = sb("ones_b", [P, P], BF16)
        xTs = sb("xTs", [P, D])
        mean_rstd = sb("mean_rstd", [P, 2, 56])
        r16 = sb("r16", [P, NT])
        rdeg = sb("rdeg", [P, NT])
        brows = sb("brows", [P, HIDDEN + D], BF16)
        small = sb("small", [P, 200])
        Wr_s = sb("Wr_s", [P, DC, EXPERTS])
        cnt = sb("cnt", [P, EXPERTS], BF16)
        used = [0]

        def tiny(n):
            used[0] += n
            assert used[0] <= 200
            return small[:, used[0] - n:used[0]]

        q_s = lend("b", HID)
        qT_s = lend("b", HID)
        o_s = lend("b", D)
        b_s = lend("b", D)
        u_s = lend("b", D)
        bacc = lend("b", HIDDEN)
        bres = lend("b", HIDDEN + D)
        b2s = lend("b", D)
        w_qu = lend("b", DC * (HID + D)).rearrange("p (c n) -> p c n", c=DC)
        bg_bc, bo_bc, go_bc, M2, sB = (lend("b", D) for _ in range(5))
        drow_flat = lend("b", P * STEPS_J)[0:1, :]
        drow = drow_flat.rearrange("o (b k) -> o b k", k=STEP_BLOCK)
        packf = o_s[0:1, 0:P * STEPS_J // STEP_BLOCK]
        pack = drow_flat[:, 0:P * STEPS_J // STEP_BLOCK].bitcast(I32)
        cmpb = lend("b", 14 * 32).bitcast(BF16).rearrange("p (j d) -> p j d", j=14)
        sqj = lend("b", D)
        bsplit = lend("b", (HIDDEN + D) // 2).bitcast(BF16)
        bu3 = [lend("c", 3 * 2 * D).rearrange("p (t w) -> p t w", w=2 * D) for _ in range(2)]
        h3 = [lend("c", 3 * D).rearrange("p (t w) -> p t w", w=D) for _ in range(2)]
        hT3 = [lend("c", 3 * D).rearrange("p (t w) -> p t w", w=D) for _ in range(2)]
        pay = [lend("c", 3 * PAYW).rearrange("p (t w) -> p t w", w=PAYW) for _ in range(2)]
        moe_at = [0]

        def inacc(n):
            moe_at[0] += n
            assert moe_at[0] <= (NT + 1) * ACCW
            return acc_flat[:, moe_at[0] - n:moe_at[0]]
        xe = [inacc(PAYW) for _ in range(2)]
        xeT = [inacc(D) for _ in range(2)]
        hs = [inacc(HIDDEN) for _ in range(2)]
        hsT = [inacc(HIDDEN) for _ in range(2)]
        ys = [inacc(D) for _ in range(2)]
        wid = [inacc(PAYW - D) for _ in range(2)]
        nid = [inacc(2)[:, 0:1].bitcast(I32) for _ in range(2)]
        moetab = inacc(2 * P)[0:1, :].bitcast(I32)
        sel = inacc(EXPERTS * P // 2).bitcast(BF16).rearrange("p (e n) -> p e n", n=P)

        pcol = tiny(1)
        pm = tiny(1)
        gpre = tiny(DC)
        svals = tiny(STEPS_J)
        eoff = tiny(EXPERTS)
        iota8 = tiny(EXPERTS)
        padpos = tiny(EXPERTS)
        padpos_i = tiny(EXPERTS).bitcast(I32)
        idcol = tiny(NT)
        br_bc = tiny(EXPERTS)
        lng = tiny(EXPERTS * DC)
        lnb = tiny(EXPERTS * DC).rearrange("p (c e) -> p c e", c=DC)
        small2 = sb("small2", [P, 316])
        used2 = [0]

        def tiny2(n):
            used2[0] += n
            assert used2[0] <= 316
            return small2[:, used2[0] - n:used2[0]]
        cend = tiny2(NT)
        ecol = tiny2(STEPS_J)
        ecol_i = tiny2(STEPS_J).bitcast(I32)
        idx = [tiny2(STEP_BLOCK).bitcast(I32) for _ in range(2)]
        dcol = tiny2(STEPS_J)
        d128 = tiny2(STEPS_J)
        ones49 = tiny2(NT)
        var49 = tiny2(NT)
        t49 = tiny2(NT)
        bst6 = tiny2(6 * 6).rearrange("p (t s) -> p t s", s=6)
        mv6 = tiny2(6).rearrange("p (t k) -> p t k", k=2)
        kmem = tiny2(MEM)
        km1 = tiny2(1)
        km2 = tiny2(1)
        rS = tiny2(1)
        qm = tiny2(HEADS)
        qsum = tiny2(HEADS)
        rq = tiny2(HEADS)
        ssB = tiny2(1)
        nrmB = tiny2(1)
        rnB = tiny2(1)
        small3 = lend("c", 390)
        used3 = [0]

        def tiny3(*shape):
            n = 1
            for k in shape:
                n *= k
            used3[0] += n
            assert used3[0] <= 390
            v = small3[:, used3[0] - n:used3[0]]
            return v.rearrange("p (a b) -> p a b", b=shape[1]) if len(shape) == 2 else v
        U = []
        for h in range(2):
            U.append(dict(
                ss=tiny3(3), nrm=tiny3(3), rn=tiny3(3), st=tiny3(3, 6), mv=tiny3(3, 2), ve=tiny3(3), sd=tiny3(3),
                rstd=tiny3(3), t2=tiny3(3), sd2=tiny3(3), r2=tiny3(3), lg=tiny3(3, 8), mx=tiny3(3, 8),
                ix=tiny3(3, 8), ixf=tiny3(3, 2), dl=tiny3(3), e2=tiny3(3), w1=tiny3(3), w2=tiny3(3),
                posf=tiny3(3, 2), posi=tiny3(3, 2)))
        small4 = sb("small4", [P, 2 * 3 * 8 * 6])
        for h in range(2):
            for k, nm in enumerate(("oh1", "oh2", "wv", "wt", "rk", "pp")):
                o = (h * 6 + k) * 24
                U[h][nm] = small4[:, o:o + 24].rearrange("p (a b) -> p a b", b=8)
            U[h]["M"] = sb(f"picked{h}", [P, 3, 8], BF16)
            U[h]["dc"] = sb(f"dcnt{h}", [P, 8])

        bank = [ctx.enter_context(nc.psum_tensor(f"bank{i}", [P, 512], F32)) for i in range(8)]

        names = """consts_pool consts_dve weights_in dve_links act_links edges_written edges_in
            stat_ready sd_ready rstd_ready sel_ready xcopy zcopy
            cmp_ready counts_ready ecol_ready step_rows_out drow_in steps_in stepsf_ready stepT_ready tables_ready
            s_built p_ready acc_done idx_ready waits_passed
            xa_in kv_mm kv_act kv_dve kmaxT km_ready kmaxrowT kmaxrow_ready mk_exp ek_sub ek_exp ctx_mm
            ctx_ready ctxT_mm ctxT_ready M2_mm M2_ready
            xb_in sb_in qu_mm qu_evac q_sub q_exp q_ready qT_mm qT_sb o_mm o_evac o_nrm bu_ready bu_out u_out
            w1_in bf_mm bf_evac fold_done brows_ready late_in
            mtab_cnt mtab_ready mtab_out moetab_in zrows""".split()
        s = {n: sem(n) for n in names}
        pair = {n: [sem(f"{n}{h}") for h in range(2)] for n in (
            "x_in", "xn_ready", "s_ready", "xnT_mm", "xnT_ready", "z_mm", "z_ready", "z_out", "xnT_out", "s_out",
            "bu_in", "y_ready", "nrm_ready", "x1_ready", "ve_ready", "sdr", "h_ready", "sd2r", "hT_mm", "hT_ready",
            "lg_mm", "pick_ready", "e2_ready", "rank_mm", "pay_ready", "scat", "x1_out", "t2_ready",
            "xe_in", "xeT_mm", "xeT_ready", "h_mm", "gelu", "hsT_mm", "hsT_dve", "hsT_act", "y_mm", "ys_ready", "y_add")}
        g_in = [sem(f"g_in{k}") for k in range(STEP_BLOCK)]

        UN = 8
        x_t = x[0:(NT - 1) * P, :].rearrange("(t p) d -> p t d", p=P)
        z_t = z_d.rearrange("(t p) d -> p t d", p=P)
        xnT_t = xnT_d.rearrange("t p d -> p t d")
        s_t = s_d.rearrange("t p d -> p t d")
        bu_t = bu_d.rearrange("t p d -> p t d")
        out_t = out.rearrange("(t p) d -> p t d", p=P)

        def units(body_iter, eng, links):
            repeat(eng, links, body_iter, 0, UN)

        def load_w2(eng, first, end, done):
            for e in range(first, end):
                eng.dma_start(w2s[:, e * HC * D:(e + 1) * HC * D].rearrange("p (c n) -> p c n", c=HC),
                              W2[e].rearrange("(c p) n -> p c n", p=P)).then_inc(done, 16)

        block = ctx.enter_context(nc.Block())

        @block.sync
        def _(sp):
            def load_x(i):
                for h in range(2):
                    until(sp, pair["x_in"][h], 16 * i)
                    sp.dma_start(x_all[:, ds(6 * i + 3 * h, 3), :], x_t[:, ds(6 * i + 3 * h, 3), :]).then_inc(pair["x_in"][h], 16)
            units(load_x, sp, None)
            sp.wait_ge(s["consts_dve"], 1)
            sp.wait_ge(pair["x_in"][0], 16 * UN)
            sp.dma_start(x_all[0:TAIL, NT - 1, :], x[(NT - 1) * P:N, :]).then_inc(pair["x_in"][0], 16)
            sp.wait_ge(s["ecol_ready"], 1)
            sp.dma_start(step_d.rearrange("(p j) -> p j", j=STEPS_J), dcol).then_inc(s["step_rows_out"], 16)
            sp.wait_ge(s["step_rows_out"], 16)
            sp.dma_start(drow, step_d.rearrange("(o b k) -> o b k", o=1, k=STEP_BLOCK)).then_inc(s["drow_in"], 16)

            def store_unit(i, h, t0, nt):
                sp.wait_ge(pair["s_ready"][h], i + 1)
                sp.dma_start(s_t[:, ds(t0, nt), :], ss[h][:, 0:nt, :]).then_inc(pair["s_out"][h], 16)
                sp.wait_ge(pair["xnT_ready"][h], i + 1)
                sp.dma_start(xnT_t[:, ds(t0, nt), :], xnT[h][:, 0:nt, :]).then_inc(pair["xnT_out"][h], 16)
                sp.wait_ge(pair["z_ready"][h], i + 1)
                sp.dma_start(z_t[:, ds(t0, nt), :], zs[h][:, 0:nt, :]).then_inc(pair["z_out"][h], 16)

            def stores(i):
                for h in range(2):
                    store_unit(i, h, 6 * i + 3 * h, 3)
            units(stores, sp, None)
            store_unit(UN, 0, NT - 1, 1)
            for h in range(2):
                sp.wait_ge(pair["xnT_out"][h], 16 * (UN + 1 - h))
                sp.wait_ge(pair["s_out"][h], 16 * (UN + 1 - h))

            def load_a(t):
                until(sp, s["kv_mm"], t)
                sp.dma_start(xTs[:, :], xnT_d[ds(t, 1)].rearrange("o p d -> (o p) d")).then_inc(s["xa_in"], 16)
            repeat(sp, None, load_a, 0, NT - 1)
            load_a(NT - 1)
            sp.wait_ge(s["kv_mm"], NT)
            sp.dma_start(xTs[:, :], xnT_d[0]).then_inc(s["xb_in"], 16)
            sp.dma_start(sB[:, :], s_d[0]).then_inc(s["sb_in"], 16)

            def store_b(t):
                sp.wait_ge(s["bu_ready"], t + 1)
                sp.dma_start(bu_d[ds(t, 1), :, 0:D].rearrange("o p d -> (o p) d"), b_s).then_inc(s["bu_out"], 16)

            def io_b(t, first=False, last=False):
                if not last:
                    sp.wait_ge(s["qu_mm"], t + 1)
                    sp.dma_start(xTs[:, :], xnT_d[ds(t + 1, 1)].rearrange("o p d -> (o p) d")).then_inc(s["xb_in"], 16)
                sp.wait_ge(s["qu_evac"], t + 1)
                sp.dma_start(bu_d[ds(t, 1), :, D:2 * D].rearrange("o p d -> (o p) d"), u_s).then_inc(s["u_out"], 16)
                if not first:
                    store_b(t - 1)
                    sp.dma_start(sB[:, :], s_d[ds(t, 1)].rearrange("o p d -> (o p) d")).then_inc(s["sb_in"], 16)

            def io_load(t, to, frm):
                io_b(t)
                sp.dma_start(to, frm).then_inc(s["w1_in"], 16)

            def w1_of(e):
                return (w1s[:, ds(e * (DC * HIDDEN), DC * HIDDEN)].rearrange("p (c n) -> p c n", c=DC),
                        W1[ds(e, 1)].rearrange("o (c p) n -> p (o c) n", p=P))

            def w2_of(e):
                return (w2s[:, ds(e * (HC * D), HC * D)].rearrange("p (c n) -> p c n", c=HC),
                        W2[ds(e, 1)].rearrange("o (c p) n -> p (o c) n", p=P))
            io_b(0, first=True)
            sp.wait_ge(s["M2_ready"], 1)
            repeat(sp, None, lambda t: io_load(t, *w1_of(t - 1)), 1, EXPERTS + 1)
            repeat(sp, None, lambda t: io_load(t, *w2_of(t - EXPERTS - 1)), EXPERTS + 1, EXPERTS + 1 + EXPERTS // 2)
            repeat(sp, None, io_b, EXPERTS + 1 + EXPERTS // 2, NT - 1)
            io_b(NT - 1, last=True)
            store_b(NT - 1)
            sp.wait_ge(s["u_out"], 16 * NT)
            sp.wait_ge(s["bu_out"], 16 * NT)

            sp.wait_ge(s["brows_ready"], 1)

            def load_u(i, h, t0, nt):
                until(sp, pair["x1_out"][h], 16 * i)
                until(sp, pair["h_ready"][h], i)
                sp.dma_start(bu3[h][:, 0:nt, :], bu_t[:, ds(t0, nt), :]).then_inc(pair["bu_in"][h], 16)

            def store_x1(i, h, t0, nt):
                sp.wait_ge(pair["x1_ready"][h], i + 1)
                sp.dma_start(out_t[:, ds(t0, nt), :], bu3[h][:, 0:nt, 0:D]).then_inc(pair["x1_out"][h], 16)

            def route_io(i):
                for h in range(2):
                    load_u(i, h, 6 * i + 3 * h, 3)
                for h in range(2):
                    store_x1(i, h, 6 * i + 3 * h, 3)
            units(route_io, sp, None)
            load_u(UN, 0, NT - 1, 1)
            store_x1(UN, 0, NT - 1, 1)
            sp.wait_ge(s["mtab_ready"], 1)
            sp.dma_start(moetab_d.rearrange("k p -> p k"), U[0]["posi"][:, 0, :].bitcast(I32),
                         allow_slow_non_contiguous=True).then_inc(s["mtab_out"], 16)
            sp.wait_ge(s["mtab_out"], 16)
            sp.dma_start(moetab[0:1, :], moetab_d.rearrange("(o k) p -> o (k p)", o=1)).then_inc(s["moetab_in"], 16)
            sp.wait_ge(s["zrows"], 16 * (EXPERTS + 2))
            for h in range(2):
                sp.wait_ge(pair["scat"][h], 16 * (6 * UN + 2 * (1 - h)))
            sp.wait_ge(s["moetab_in"], 16)

            def load_xe(i, h):
                r = sp.value_load(moetab[0:1, ds(2 * i + h, 1)], min_val=0, max_val=PADROW)
                until(sp, pair["xeT_ready"][h], i)
                sp.dma_start(xe[h][:, :], bucket_d[ds(r, P), :]).then_inc(pair["xe_in"][h], 16)
            load_xe(0, 0)
            load_xe(0, 1)

            def load_xes(i):
                for h in range(2):
                    load_xe(i, h)
            with sp.Fori(1, MOE_TILES // 2) as i:
                load_xes(i)
            for h in range(2):
                sp.wait_ge(pair["y_add"][h], 16 * (MOE_TILES // 2))

        @block.gpsimd
        def _(pool):
            def iota_f(ap, pattern, base, mult):
                return pool.iota(ap, pattern=pattern, base=base, channel_multiplier=mult, allow_small_or_imprecise_dtypes=True)
            iota_f(iota[:, :], [[1, P]], 0, 0)
            iota_f(pcol, [[0, 1]], 0, 1)
            iota_f(thrL, [[P, NT]], 0, 0)
            iota_f(thrF, [[P, NT]], P, 0)
            iota_f(svals, [[1, STEPS_J]], 0, STEPS_J)
            iota_f(eoff, [[CAP, EXPERTS]], 0, 0)
            iota_f(iota8, [[1, EXPERTS]], 0, 0)
            iota_f(padpos, [[CAP, EXPERTS]], 0, 1)
            iota_f(idcol, [[P, NT]], 0, 1).then_inc(s["consts_pool"], 1)

            def add_unit(i, h, t0, nt):
                pool.wait_ge(pair["xn_ready"][h], i + 1)
                until(pool, pair["s_out"][h], 16 * i)
                pool.tensor_tensor(ss[h][:, 0:nt, :], x_all[:, ds(t0, nt), :], xn[h][:, 0:nt, :], ALU.add).then_inc(pair["s_ready"][h], 1)

            def adds(i):
                for h in range(2):
                    add_unit(i, h, 6 * i + 3 * h, 3)
            def step_rows():
                pool.wait_ge(s["ecol_ready"], 1)
                for j in range(STEPS_J):
                    pool.indirect_dma_start(out=steps_e[:, j].rearrange("p k e -> p (k e)"), out_offset=None,
                                            in_=edges_d.rearrange("r k e -> r (k e)"),
                                            in_offset=bass.IndirectOffsetOnAxis(ap=ecol_i[:, j:j + 1], axis=0)
                                            ).then_inc(s["steps_in"], 16)
            adds(0)
            step_rows()
            with pool.Fori(1, UN) as i:
                adds(i)
            add_unit(UN, 0, NT - 1, 1)

            pool.wait_ge(s["tables_ready"], 2)
            for h in range(2):
                pool.wait_ge(pair["z_out"][h], 16 * (UN + 1 - h))

            def copy_idx(b, half):
                pool.tensor_copy(idx[half], srcT[:, ds(STEP_BLOCK * b, STEP_BLOCK)]).then_inc(s["idx_ready"], 1)

            def gather_block(b, half, last=False):
                pool.wait_ge(s["idx_ready"], b + 1)
                for k in range(STEP_BLOCK):
                    until(pool, s["p_ready"], STEP_BLOCK * (b - 1) + k + 1)
                    if k == STEP_BLOCK - 1 and not last:
                        copy_idx(b + 1, 1 - half)
                    else:
                        stand_alone(pool, s["waits_passed"])
                    pool.indirect_dma_start(out=G[:, k, 0:D], out_offset=None, in_=z_d[:, :],
                                            in_offset=bass.IndirectOffsetOnAxis(ap=idx[half][:, k:k + 1], axis=0)
                                            ).then_inc(g_in[k], 16)
            copy_idx(0, 0)
            gather_block(0, 0)
            with pool.Fori(0, BLOCKS // 2 - 1) as i:
                gather_block(2 * i + 1, 1)
                gather_block(2 * i + 2, 0)
            gather_block(BLOCKS - 1, 1, True)

            def scatter_unit(i, h, nt, rows):
                pool.wait_ge(pair["pay_ready"][h], i + 1)
                stand_alone(pool, s["waits_passed"])
                for tt in range(nt):
                    for c in range(2):
                        pool.indirect_dma_start(out=bucket_d[:, :],
                                                out_offset=bass.IndirectOffsetOnAxis(ap=U[h]["posi"].bitcast(I32)[0:rows, tt, c:c + 1], axis=0),
                                                in_=pay[h][0:rows, tt, :], in_offset=None).then_inc(pair["scat"][h], 16)

            def scatters(i):
                for h in range(2):
                    scatter_unit(i, h, 3, P)
            repeat(pool, None, scatters, 0, UN)
            scatter_unit(UN, 0, 1, TAIL)
            pool.wait_ge(s["mtab_ready"], 1)
            for e in range(EXPERTS):
                pool.indirect_dma_start(out=bucket_d[:, :], out_offset=bass.IndirectOffsetOnAxis(ap=padpos_i[:, e:e + 1], axis=0),
                                        in_=pay[1][:, 0, :], in_offset=None).then_inc(s["zrows"], 16)
            pool.dma_start(bucket_d[PADROW:PADROW + P, :], pay[1][:, 0, :]).then_inc(s["zrows"], 16)
            pool.dma_start(out[NT * P:NT * P + P, :], pay[1][:, 0, 0:D]).then_inc(s["zrows"], 16)
            for h in range(2):
                pool.wait_ge(pair["x1_out"][h], 16 * (UN + 1 - h))
            pool.wait_ge(s["zrows"], 16 * (EXPERTS + 2))

            def add_y(i, h):
                pool.wait_ge(pair["ys_ready"][h], i + 1)
                until(pool, pair["y_add"][1 - h], 16 * (i + h))
                stand_alone(pool, s["waits_passed"])
                pool.indirect_dma_start(out=out[:, :], out_offset=bass.IndirectOffsetOnAxis(ap=nid[h], axis=0),
                                        in_=ys[h], in_offset=None, compute_op=ALU.add).then_inc(pair["y_add"][h], 16)

            def adds_y(i):
                for h in range(2):
                    add_y(i, h)
            repeat(pool, None, adds_y, 0, MOE_TILES // 2)

        @block.scalar
        def _(act):
            L = Links(act, s["act_links"])
            w = s["edges_written"]
            act.dma_start(edges_d[0:EFULL, 0, :], src[0:EFULL * P].rearrange("(r e) -> r e", e=P)).then_inc(w, 16)
            act.dma_start(edges_d[0:EFULL, 1, :], dst[0:EFULL * P].rearrange("(r e) -> r e", e=P)).then_inc(w, 16)
            act.dma_start(edges_d[EFULL:EFULL + 1, 0, 0:EREST], src[EFULL * P:EDGES].rearrange("(r e) -> r e", r=1)).then_inc(w, 16)
            act.dma_start(edges_d[EFULL:EFULL + 1, 1, 0:EREST], dst[EFULL * P:EDGES].rearrange("(r e) -> r e", r=1)).then_inc(w, 16)
            act.wait_ge(s["consts_dve"], 1)
            nr = EROWS - EFULL - 1
            act.dma_start(edges_d[EFULL:EFULL + 1, 0, EREST:P], epad[0:1, 0:P - EREST]).then_inc(w, 16)
            act.dma_start(edges_d[EFULL:EFULL + 1, 1, EREST:P], epad[0:1, D:D + P - EREST]).then_inc(w, 16)
            act.dma_start(edges_d[EFULL + 1:EROWS, 0, :], epad[0:1, 0:nr * P].rearrange("p (r e) -> p r e", e=P)).then_inc(w, 16)
            act.dma_start(edges_d[EFULL + 1:EROWS, 1, :], epad[0:1, D:D + nr * P].rearrange("p (r e) -> p r e", e=P)).then_inc(w, 16)
            act.wait_ge(w, 8 * 16)
            act.dma_start(ed[0:EP], edges_d.rearrange("(p j) k e -> p j k e", j=EJ)).then_inc(s["edges_in"], 16)
            n_w = 0
            for to, frm in ((w_neigh, gnn_W[D:2 * D, :].rearrange("(c p) n -> p c n", p=P)),
                            (w_qu[:, :, HID:HID + D], gnn_W[0:D, :].rearrange("(c p) n -> p c n", p=P)),
                            (w_qu[:, :, 0:HID], w_qkv[:, 0:HID].rearrange("(c p) n -> p c n", p=P)),
                            (w_kv, w_qkv[:, HID:3 * HID].rearrange("(c p) n -> p c n", p=P)),
                            (bg_bc[:, :], gnn_b.rearrange("(o d) -> o d", o=1).to_broadcast([P, D])),
                            (bo_bc[:, :], b_out.rearrange("(o d) -> o d", o=1).to_broadcast([P, D])),
                            (go_bc[:, :], g_out.rearrange("(o d) -> o d", o=1).to_broadcast([P, D])),
                            (br_bc, br.rearrange("(o d) -> o d", o=1).to_broadcast([P, EXPERTS])),
                            (w_outs, w_out[:, :]),
                            (kmem, mem_kv[0].rearrange("h d m -> (h d) m")),
                            (Wr_s[:, :, :], Wr.rearrange("(c p) n -> p c n", p=P)),
                            (bacc[0:EXPERTS, :], b1[:, :]),
                            (b2s[0:EXPERTS, :], b2[:, :])):
                act.dma_start(to, frm).then_inc(s["weights_in"], 16)
                n_w += 1
            with nc.allow_non_contiguous_dma(reason="small parameters, transposed once"):
                for c in range(DC):
                    act.dma_start(gpre[:, c:c + 1], g_pre[c * P:(c + 1) * P].rearrange("(p o) -> p o", o=1)).then_inc(s["weights_in"], 16)
                    act.dma_start(lng.rearrange("p (e c) -> p e c", c=DC)[:, :, c:c + 1],
                                  ln_g[:, c * P:(c + 1) * P].rearrange("e (p o) -> p e o", o=1)).then_inc(s["weights_in"], 16)
                    act.dma_start(lnb[:, c, :], ln_b[:, c * P:(c + 1) * P].rearrange("e p -> p e")).then_inc(s["weights_in"], 16)
                act.dma_start(mkT[:, :], mem_kv[0].rearrange("h d m -> m (h d)")).then_inc(s["weights_in"], 16)
                act.dma_start(mv1[:, 0:HID], mem_kv[1].rearrange("h d m -> m (h d)")).then_inc(s["weights_in"], 16)
            assert n_w + 3 * DC + 2 == N_WEIGHTS

            act.wait_ge(s["stat_ready"], 1)
            act.activation(mean_rstd[:, 1, 0:NT], var49, ACT.Sqrt).then_inc(s["sd_ready"], 1)
            act.wait_ge(s["rstd_ready"], 1)
            act.activation(r16[:, :], t49, ACT.Sqrt).then_inc(s["sd_ready"], 1)

            def copy_xnT(i, h, nt):
                for tt in range(nt):
                    act.wait_ge(pair["xnT_mm"][h], 3 * i + tt + 1)
                    if tt == 0:
                        until(act, pair["xnT_out"][h], 16 * i)
                        until(act, pair["z_mm"][h], 3 * i)
                    c = act.activation(xnT[h][:, tt, :], bank[tt][:, 0:D], ACT.Copy)
                    c.then_inc(pair["xnT_ready"][h] if tt == nt - 1 else s["xcopy"], 1)

            def copies(i):
                for h in range(2):
                    copy_xnT(i, h, 3)
            repeat(act, None, copies, 0, UN)
            copy_xnT(UN, 0, 1)

            def kv(t):
                act.wait_ge(s["kv_mm"], t + 1)
                act.activation(kv_all[:, ds(t, 1), 0:2 * HID].rearrange("p o w -> p (o w)"), bank[4][:, 0:2 * HID], ACT.Copy,
                               scale=r16[:, ds(t, 1)]).then_inc(s["kv_act"], 1)
            act.wait_ge(s["rstd_ready"], 2)
            repeat(act, None, kv, 0, NT - 1)
            kv(NT - 1)
            act.wait_ge(s["kmaxrow_ready"], 1)
            act.activation(mkT[:, :], mkT[:, :], ACT.Exp).then_inc(s["mk_exp"], 1)

            def exp_k(g, nt=8, rows=P):
                act.wait_ge(s["ek_sub"], g + 1)
                act.activation(ek[0:rows, 0:nt, :], ek[0:rows, 0:nt, :], ACT.Exp).then_inc(s["ek_exp"], 1)
            repeat(act, None, exp_k, 0, 6)
            exp_k(6, 1, TAIL)

            def exp_q(t):
                act.wait_ge(s["q_sub"], t + 1)
                act.activation(q_s, q_s, ACT.Exp).then_inc(s["q_exp"], 1)

            def norm_o(t):
                act.wait_ge(s["o_evac"], t + 1)
                L.after(act.activation(sqj, o_s, ACT.Square, accum_out=ssB))
                act.activation(nrmB, ssB, ACT.Sqrt).then_inc(s["o_nrm"], 1)

            def copy_qT(t):
                act.wait_ge(s["qT_mm"], t + 1)
                until(act, s["o_mm"], t)
                act.activation(qT_s, bank[6][:, 0:P], ACT.Copy).then_inc(s["qT_sb"], 1)

            def mix(t):
                exp_q(t)
                norm_o(t - 1)
                copy_qT(t)

            def mix_and_fold(t):
                mix(t)
                j = t - 24
                if isinstance(t, int):
                    act.wait_ge(s["bf_mm"], 2 * EXPERTS)
                w = w1s[:, ds(j * HIDDEN, HIDDEN)]
                act.activation(w, w, ACT.Copy, scale=lng[:, ds(j, 1)]).then_inc(s["fold_done"], 1)
            exp_q(0)
            copy_qT(0)
            repeat(act, L, mix, 1, 24)
            repeat(act, L, mix_and_fold, 24, 40)
            repeat(act, L, mix, 40, NT)
            norm_o(NT - 1)

            def r_relu(i, h, nt):
                u = U[h]
                act.wait_ge(pair["y_ready"][h], i + 1)
                y = bu3[h][:, 0:nt, D:2 * D]
                L.after(act.activation(y, y, ACT.Relu))
                for tt in range(nt):
                    a = act.activation(G[:, 3 * h + tt, 0:D], y[:, tt, :], ACT.Square, accum_out=u["ss"][:, tt:tt + 1])
                L.after(a)
                act.activation(u["nrm"][:, 0:nt], u["ss"][:, 0:nt], ACT.Sqrt).then_inc(pair["nrm_ready"][h], 1)

            def r_sd(i, h, nt):
                u = U[h]
                act.wait_ge(pair["ve_ready"][h], i + 1)
                act.activation(u["sd"][:, 0:nt], u["ve"][:, 0:nt], ACT.Sqrt).then_inc(pair["sdr"][h], 1)

            def r_sd2(i, h, nt):
                u = U[h]
                act.wait_ge(pair["t2_ready"][h], i + 1)
                act.activation(u["sd2"][:, 0:nt], u["t2"][:, 0:nt], ACT.Sqrt).then_inc(pair["sd2r"][h], 1)

            def r_hT(i, h, nt):
                act.wait_ge(pair["hT_mm"][h], i + 1)
                for tt in range(nt):
                    c = act.activation(hT3[h][:, tt, :], bank[2 * h + tt // 2][:, (tt % 2) * D:(tt % 2 + 1) * D], ACT.Copy)
                c.then_inc(pair["hT_ready"][h], 1)

            def r_e2(i, h, nt):
                u = U[h]
                act.wait_ge(pair["pick_ready"][h], i + 1)
                act.activation(u["e2"][:, 0:nt], u["dl"][:, 0:nt], ACT.Exp).then_inc(pair["e2_ready"][h], 1)

            def route(i):
                for f in (r_relu, r_sd, r_sd2, r_hT, r_e2):
                    for h in range(2):
                        f(i, h, 3)
            repeat(act, L, route, 0, UN)
            for f in (r_relu, r_sd, r_sd2, r_hT, r_e2):
                f(UN, 0, 1)
            for h in range(2):
                act.wait_ge(pair["x1_out"][h], 16 * (UN + 1 - h))
                act.wait_ge(pair["scat"][h], 16 * (6 * UN + 2 * (1 - h)))
            act.wait_ge(s["moetab_in"], 16)
            act.wait_ge(s["zrows"], 16 * (EXPERTS + 2))
            load_w2(act, EXPERTS // 2, EXPERTS, s["late_in"])

            def gelu(i, h):
                for n in range(2):
                    act.wait_ge(pair["h_mm"][h], 2 * i + n + 1)
                    if n == 0:
                        until(act, pair["hsT_mm"][h], 2 * i)
                    act.activation(hs[h][:, n * 512:(n + 1) * 512], bank[2 + n][:, :], ACT.Gelu).then_inc(pair["gelu"][h], 1)

            def copy_hsT(i, h):
                act.wait_ge(pair["hsT_mm"][h], 2 * i + 2)
                until(act, pair["y_mm"][h], i)
                act.activation(hsT[h][:, 512:1024], bank[5][:, :], ACT.Copy).then_inc(pair["hsT_act"][h], 1)
            gelu(0, 0)

            def moe(i, last=False):
                copy_hsT(i, 0)
                gelu(i, 1)
                copy_hsT(i, 1)
                if not last:
                    gelu(i + 1, 0)
            repeat(act, None, moe, 0, MOE_TILES // 2 - 1)
            moe(MOE_TILES // 2 - 1, True)

        @block.vector
        def _(dve):
            L = Links(dve, s["dve_links"])
            dve.memset(epad[0:1, 0:D], 0)
            dve.memset(epad[0:1, D:2 * D], NOWHERE)
            dve.memset(x_all[:, NT - 1, :], 0.0).then_inc(s["consts_dve"], 1)
            dve.memset(acc_flat, 0.0)
            dve.memset(G[:, :, D:ACCW], 1.0)
            dve.memset(ones_b[:, :], 1.0)
            dve.memset(ones49, 1.0)
            dve.memset(cnt[:, :], 0.0)
            dve.memset(brows[:, :], 0.0)
            dve.memset(mv1[:, HID:HID + 2], 1.0)
            dve.memset(headmask, 0.0)
            L.after(dve.memset(delta[:, NT - 1:NT], float(EROWS)))
            for hd in range(HEADS):
                a = dve.memset(headmask[hd * HD:(hd + 1) * HD, hd * HD:(hd + 1) * HD], SCALE)
            L.after(a)
            dve.wait_ge(s["consts_pool"], 1)
            dve.tensor_scalar(ident[:, :], iota[:, :], pcol, None, ALU.is_equal).then_inc(s["consts_dve"], 1)
            dve.tensor_scalar(before[:, :], iota[:, :], pcol, None, ALU.is_gt)
            for k in range(3):
                a = dve.tensor_scalar(pm[32 * k:32 * k + 32], pcol[32 * k:32 * k + 32], -32.0 * k, None, ALU.add)
            L.after(a)
            dve.wait_ge(s["weights_in"], 16 * N_WEIGHTS)
            for c in range(DC):
                dve.tensor_scalar(w_kv[:, c, :], w_kv[:, c, :], gpre[:, c:c + 1], None, ALU.mult)
                dve.tensor_scalar(w_qu[:, c, 0:HID], w_qu[:, c, 0:HID], gpre[:, c:c + 1], None, ALU.mult)
            dve.tensor_scalar(go_bc[:, :], go_bc[:, :], float(D) ** 0.5, None, ALU.mult).then_inc(s["consts_dve"], 1)

            def stats(t, nt):
                for tt in range(nt):
                    a = dve.bn_stats(bst6[:, tt, :], x_all[:, ds(t + tt, 1), :].rearrange("p o d -> p (o d)"))
                L.after(a)
                stand_alone(dve, s["waits_passed"])
                for tt in range(nt):
                    a = dve.bn_aggr(mv6[:, tt, :], bst6[:, tt, :])
                L.after(a)
                return dve.tensor_copy(mean_rstd[:, :, ds(t, nt)].rearrange("p k t -> p t k"), mv6[:, 0:nt, :])

            def stats_iter(i):
                for h in range(2):
                    dve.wait_ge(pair["x_in"][h], 16 * (i + 1))
                    stats(6 * i + 3 * h, 3)
            repeat(dve, L, stats_iter, 0, UN)
            dve.wait_ge(pair["x_in"][0], 16 * (UN + 1))
            L.after(stats(NT - 1, 1))
            mean, rstd = mean_rstd[:, 0, 0:NT], mean_rstd[:, 1, 0:NT]
            dve.tensor_copy(t49, rstd)
            dve.tensor_scalar(var49, rstd, EPS_LN, None, ALU.add).then_inc(s["stat_ready"], 1)
            dve.wait_ge(s["stat_ready"], 1)
            dve.wait_ge(s["sd_ready"], 1)
            L.after(dve.reciprocal(rstd, rstd))
            L.after(dve.tensor_tensor(t49, t49, rstd, ALU.mult))
            L.after(dve.tensor_tensor(t49, t49, rstd, ALU.mult))
            dve.tensor_scalar(t49, t49, float(D), None, ALU.mult).then_inc(s["rstd_ready"], 1)

            def norm_unit(i, h, t0, nt):
                until(dve, pair["xnT_mm"][h], 3 * i)
                until(dve, pair["s_ready"][h], i)
                for tt in range(nt):
                    a = dve.tensor_scalar(xn[h][:, tt, :], x_all[:, ds(t0 + tt, 1), :].rearrange("p o d -> p (o d)"),
                                          mean_rstd[:, 0, ds(t0 + tt, 1)], mean_rstd[:, 1, ds(t0 + tt, 1)],
                                          ALU.subtract, ALU.mult)
                a.then_inc(pair["xn_ready"][h], 1)

            def z_unit(i, h, nt):
                for tt in range(nt):
                    dve.wait_ge(pair["z_mm"][h], 3 * i + tt + 1)
                    if tt == 0:
                        until(dve, pair["z_out"][h], 16 * i)
                    a = dve.tensor_copy(zs[h][:, tt, :], bank[3 + tt][:, 0:D])
                    if tt < nt - 1:
                        a.then_inc(s["zcopy"], 1)
                a.then_inc(pair["z_ready"][h], 1)

            def norm_iter(i):
                for h in range(2):
                    norm_unit(i, h, 6 * i + 3 * h, 3)
                for h in range(2):
                    z_unit(i, h, 3)

            def step_tables():
                dve.wait_ge(s["edges_in"], 16)
                fl = firstlast.rearrange("p (k j) -> p k j", k=2)
                dve.tensor_copy(fl[0:EP, 0, :], ed[0:EP, :, 1, P - 1:P].rearrange("p j o -> p (j o)"))
                L.after(dve.tensor_copy(fl[0:EP, 1, :], ed[0:EP, :, 1, 0:1].rearrange("p j o -> p (j o)")))
                for k, thr in ((0, thrL), (1, thrF)):
                    for j in range(EJ):
                        a = dve.tensor_scalar(cmpb[0:EP, k * EJ + j, 0:NT], thr[0:EP], fl[0:EP, k, j:j + 1], None, ALU.is_gt)
                a.then_inc(s["cmp_ready"], 1)
                dve.wait_ge(s["counts_ready"], 2)
                dve.tensor_copy(Lr[:, 0:NT], bank[6][:, 0:NT])
                L.after(dve.tensor_copy(Fr, bank[7][:, 0:NT]))
                L.after(dve.tensor_tensor(cr, Fr, Lr[:, 0:NT], ALU.subtract))
                L.after(dve.tensor_scalar(pairs, cr, 1.0, None, ALU.add))
                L.after(dve.tensor_scalar(pairs, pairs, 1, None, ALU.logical_shift_right))
                L.after(dve.tensor_scalar(cr, pairs, 2.0, None, ALU.mult))
                L.after(dve.tensor_tensor_scan(cend, ones49, cr, 0.0, ALU.mult, ALU.add))
                L.after(dve.tensor_tensor(Fr, Lr[:, 0:NT], cr, ALU.add))
                L.after(dve.tensor_tensor(delta[:, 0:NT - 1], Lr[:, 1:NT], Fr[:, 0:NT - 1], ALU.subtract))
                for j in range(STEPS_J):
                    L.after(dve.scalar_tensor_tensor(out=junk49, in0=cend, scalar=svals[:, j:j + 1], in1=delta,
                                                     op0=ALU.is_le, op1=ALU.mult, accum_out=ecol[:, j:j + 1]))
                    L.after(dve.scalar_tensor_tensor(out=junk49, in0=cend, scalar=svals[:, j:j + 1], in1=ones49,
                                                     op0=ALU.is_le, op1=ALU.mult, accum_out=dcol[:, j:j + 1]))
                L.after(dve.tensor_tensor(ecol, ecol, svals, ALU.add))
                dve.tensor_scalar(ecol_i, ecol, float(EROWS - 1), None, ALU.min)
                dve.tensor_scalar(d128, dcol, float(P), None, ALU.mult).then_inc(s["ecol_ready"], 1)
            before_loop = L.count
            norm_iter(0)
            per = L.count - before_loop
            assert per == 0
            step_tables()
            with dve.Fori(1, UN) as i:
                norm_iter(i)
            norm_unit(UN, 0, NT - 1, 1)
            z_unit(UN, 0, 1)
            dve.wait_ge(s["sd_ready"], 2)
            L.after(dve.tensor_scalar(r16[:, :], r16[:, :], TINY, None, ALU.max))
            L.after(dve.reciprocal(r16[:, :], r16[:, :]))
            dve.tensor_scalar(r16[:, :], r16[:, :], float(D) ** 0.5, None, ALU.mult).then_inc(s["rstd_ready"], 1)
            dve.wait_ge(s["steps_in"], 16 * STEPS_J)
            dve.wait_ge(s["ecol_ready"], 1)
            dve.tensor_copy(steps_f[:, :, 0, :], steps_e[:, :, 0, :])
            for j in range(STEPS_J):
                a = dve.tensor_scalar(steps_f[:, j, 1, :], steps_e[:, j, 1, :], d128[:, j:j + 1], None, ALU.subtract)
            a.then_inc(s["stepsf_ready"], 1)
            for k, tab in ((0, srcT), (1, dstT)):
                to = tab[:, :].rearrange("e (p j) -> e j p", j=STEPS_J)
                for half, (j0, j1) in enumerate(((0, 4), (4, 7))):
                    dve.wait_ge(s["stepT_ready"], 2 * k + half + 1)
                    a = dve.tensor_copy(to[:, j0:j1, :], bank[2 * k + half][:, 0:(j1 - j0) * P].rearrange("e (j p) -> e j p", p=P))
                a.then_inc(s["tables_ready"], 1)
            dve.wait_ge(s["tables_ready"], 2)
            dve.wait_ge(s["rstd_ready"], 2)
            for h in range(2):
                dve.wait_ge(pair["s_ready"][h], UN + 1 - h)
            dve.memset(kmax, -3e38)
            dve.memset(kv_all[:, :, 2 * HID:KVW], 1.0).then_inc(s["consts_dve"], 1)
            dve.wait_ge(s["drow_in"], 16)

            def pair_tile(k):
                return drow[:, :, 2 * k:2 * k + 1].rearrange("o b k -> o (b k)")
            L.after(dve.scalar_tensor_tensor(out=packf, in0=pair_tile(PAIRS - 1), scalar=float(1 << TILE_BITS),
                                             in1=pair_tile(PAIRS - 2), op0=ALU.mult, op1=ALU.add))
            for k in range(PAIRS - 3, -1, -1):
                L.after(dve.scalar_tensor_tensor(out=packf, in0=packf, scalar=float(1 << TILE_BITS), in1=pair_tile(k),
                                                 op0=ALU.mult, op1=ALU.add))
            L.after(dve.tensor_copy(pack, packf))

            def build_S(group, slot):
                dve.tensor_tensor(S[:, slot, :, :], iota[:, :].rearrange("p (o n) -> p o n", o=1).to_broadcast([P, S_GROUP, P]),
                                  dstT[:, ds(S_GROUP * group, S_GROUP)].rearrange("p (g o) -> p g o", o=1).to_broadcast([P, S_GROUP, P]),
                                  ALU.is_equal).then_inc(s["s_built"], 1)

            def walk(i, hooks={}):
                word = dve.value_load(pack[0:1, ds(i, 1)])
                for k in range(STEP_BLOCK):
                    step = STEP_BLOCK * i + k
                    if k % S_GROUP == 0:
                        until(dve, s["p_ready"], step)
                        build_S(2 * i + k // S_GROUP + 1, (k // S_GROUP + 1) % 2)
                    if k % 2:
                        pair_no = PAIRS * i + k // 2
                        dve.wait_ge(s["p_ready"], step + 1)
                        until(dve, s["acc_done"], pair_no)
                        tile = (word >> (TILE_BITS * (k // 2))) & ((1 << TILE_BITS) - 1)
                        tile = nc.s_assert_within(tile, 0, NT, skip_runtime_bounds_check_because="a count of at most NT tiles")
                        to = acc_flat[:, ds(tile * ACCW, ACCW)]
                        dve.tensor_tensor(to, to, bank[k // 2][:, 0:ACCW], ALU.add).then_inc(s["acc_done"], 1)
                    if k in hooks:
                        hooks[k]()
            build_S(0, 0)

            def kmax_tile(t, rows=P):
                dve.wait_ge(s["kv_act"], t + 1)
                until(dve, s["kv_dve"], t)
                dve.tensor_tensor(kmax[0:rows], kv_all[0:rows, ds(t, 1), 0:HID].rearrange("p o w -> p (o w)"), kmax[0:rows],
                                  ALU.max).then_inc(s["kv_dve"], 1)
            repeat(dve, L, lambda i: walk(i, {7: lambda: kmax_tile(i)}), 0, NT - 1)
            kmax_tile(NT - 1, TAIL)
            dve.wait_ge(s["kmaxT"], 1)
            dve.tensor_reduce(km1, bank[6][:, 0:P], AX, ALU.max)
            L.after(dve.tensor_reduce(km2, kmem, AX, ALU.max))
            L.after(dve.tensor_tensor(km1, km1, km2, ALU.max))
            dve.tensor_copy(kmaxb, km1.to_broadcast([P, HID])).then_inc(s["km_ready"], 1)
            dve.wait_ge(s["kmaxrowT"], 1)
            L.after(dve.tensor_copy(kmaxrow, bank[6][:, 0:P]))
            dve.tensor_tensor(mkT[:, :], mkT[:, :], kmaxrow[0:MEM], ALU.subtract).then_inc(s["kmaxrow_ready"], 1)

            def sub_k(g, nt=8, rows=P):
                until(dve, s["ctx_mm"], g + 0)
                dve.wait_ge(s["kv_act"], NT)
                dve.tensor_tensor(ek[0:rows, 0:nt, :], kv_all[0:rows, ds(8 * g, nt), 0:HID],
                                  kmaxrow[0:rows].rearrange("p (o d) -> p o d", o=1).to_broadcast([rows, nt, HID]),
                                  ALU.subtract).then_inc(s["ek_sub"], 1)
            A2 = NT - 1
            repeat(dve, L, lambda i: walk(i, {0: lambda: sub_k(i - A2)}), A2, A2 + 6)
            sub_k(6, 1, TAIL)
            dve.wait_ge(s["ctx_mm"], 7)
            L.after(dve.reciprocal(rS, bank[5][:, HID:HID + 1]))
            dve.scalar_tensor_tensor(out=ctxs, in0=bank[5][:, 0:HID], scalar=rS, in1=headmask,
                                     op0=ALU.mult, op1=ALU.mult).then_inc(s["ctx_ready"], 1)
            dve.wait_ge(s["ctxT_mm"], 1)
            dve.tensor_copy(ctxT, bank[6][:, 0:P]).then_inc(s["ctxT_ready"], 1)
            dve.wait_ge(s["M2_mm"], 1)
            dve.tensor_copy(M2[:, :], bank[7][:, 0:D]).then_inc(s["M2_ready"], 1)

            q4 = q_s.rearrange("p (h d) -> p h d", h=HEADS)

            def heads(v):
                return v.rearrange("p (h o) -> p h o", o=1).to_broadcast([P, HEADS, HD])

            def b_q1(t):
                dve.wait_ge(s["qu_mm"], t + 1)
                L.after(dve.tensor_scalar(q_s, bank[4][:, 0:HID], r16[:, ds(t, 1)], None, ALU.mult))
                L.after(dve.tensor_reduce(qm, q4, AX, ALU.max))
                dve.tensor_tensor(q4, q4, heads(qm), ALU.subtract).then_inc(s["q_sub"], 1)
                until(dve, s["u_out"], 16 * t)
                dve.tensor_tensor(u_s, bank[4][:, HID:HID + D], bg_bc[:, :], ALU.add).then_inc(s["qu_evac"], 1)

            def b_q2(t):
                dve.wait_ge(s["q_exp"], t + 1)
                L.after(dve.tensor_reduce(qsum, q4, AX, ALU.add))
                L.after(dve.reciprocal(rq, qsum))
                dve.tensor_tensor(q4, q4, heads(rq), ALU.mult).then_inc(s["q_ready"], 1)

            def b_o1(t):
                dve.wait_ge(s["o_mm"], t + 1)
                dve.tensor_tensor(o_s, bank[7][:, 0:D], bo_bc[:, :], ALU.add).then_inc(s["o_evac"], 1)

            def b_o2(t):
                dve.wait_ge(s["o_nrm"], t + 1)
                dve.wait_ge(s["sb_in"], 16 * (t + 1))
                until(dve, s["bu_out"], 16 * t)
                L.after(dve.tensor_scalar(rnB, nrmB, TINY, None, ALU.max))
                L.after(dve.reciprocal(rnB, rnB))
                L.after(dve.scalar_tensor_tensor(out=o_s, in0=o_s, scalar=rnB, in1=go_bc[:, :], op0=ALU.mult, op1=ALU.mult))
                dve.tensor_tensor(b_s, o_s, sB[:, :], ALU.add).then_inc(s["bu_ready"], 1)

            B0 = A2 + 6

            def b_hooks(t, first=False):
                hk = {0: lambda: b_q1(t), 3: lambda: b_q2(t)}
                if not first:
                    hk[1] = lambda: b_o1(t - 1)
                    hk[6] = lambda: b_o2(t - 1)
                return hk

            def b_fold(e, n):
                dve.wait_ge(s["bf_mm"], 2 * e + n + 1)
                c = bacc[0:EXPERTS, n * 512:(n + 1) * 512]
                dve.scalar_tensor_tensor(out=c, in0=bank[5][0:EXPERTS, :], scalar=ident[0:EXPERTS, ds(e, 1)],
                                         in1=c, op0=ALU.mult, op1=ALU.add).then_inc(s["bf_evac"], 1)

            def fold_hooks(t):
                hk = b_hooks(t)
                e = t - 16
                hk[4] = lambda: (until(dve, s["bf_evac"], 2 * e), b_fold(e, 0))
                hk[7] = lambda: b_fold(e, 1)
                return hk
            walk(B0, b_hooks(0, True))
            repeat(dve, L, lambda t: walk(t + B0, b_hooks(t)), 1, 16)
            repeat(dve, L, lambda t: walk(t + B0, fold_hooks(t)), 16, 24)
            repeat(dve, L, lambda t: walk(t + B0, b_hooks(t)), 24, NT)
            walk(B0 + NT, {1: lambda: b_o1(NT - 1), 6: lambda: b_o2(NT - 1)})
            for i in range(B0 + NT + 1, BLOCKS):
                walk(i)
            dve.wait_ge(s["bf_evac"], 2 * EXPERTS)
            dve.tensor_copy(bres[0:EXPERTS, 0:HIDDEN], bacc[0:EXPERTS, :])
            L.after(dve.tensor_copy(bres[0:EXPERTS, HIDDEN:HIDDEN + D], b2s[0:EXPERTS, :]))
            for k in range(3):
                to = brows[32 * k:32 * k + EXPERTS, :]
                L.after(dve.tensor_copy(brows[0:EXPERTS, :] if k == 0 else bsplit[0:EXPERTS, :], bres[0:EXPERTS, :]))
                part = brows[0:EXPERTS, :] if k == 0 else bsplit[0:EXPERTS, :]
                if k:
                    dve.tensor_copy(to, part)
                if k < 2:
                    L.after(dve.tensor_tensor(bres[0:EXPERTS, :], bres[0:EXPERTS, :], part, ALU.subtract))
            dve.wait_ge(s["acc_done"], PAIRS * BLOCKS)
            deg = acc[:, 0:NT, D:D + 1].rearrange("p t o -> p (t o)")
            L.after(dve.tensor_scalar(rdeg[:, :], deg, 1.0, None, ALU.max))
            L.after(dve.reciprocal(rdeg[:, :], rdeg[:, :]))
            dve.wait_ge(s["bu_out"], 16 * NT)
            for h in range(2):
                for tt in range(3):
                    a = dve.memset(pay[h][:, tt, ID_AT:PAYW], 0.0)
            L.after(a)
            dve.memset(U[0]["M"][:, :, :], 0.0).then_inc(s["brows_ready"], 1)

            def r_y(i, h, t0, nt, rows):
                dve.wait_ge(pair["bu_in"][h], 16 * (i + 1))
                for tt in range(nt):
                    y = bu3[h][:, tt, D:2 * D]
                    a = dve.scalar_tensor_tensor(out=y, in0=acc[:, ds(t0 + tt, 1), 0:D].rearrange("p o d -> p (o d)"),
                                                 scalar=rdeg[:, ds(t0 + tt, 1)], in1=y, op0=ALU.mult, op1=ALU.add)
                a.then_inc(pair["y_ready"][h], 1)

            def r_x1(i, h, t0, nt, rows):
                u = U[h]
                dve.wait_ge(pair["nrm_ready"][h], i + 1)
                L.after(dve.tensor_scalar(u["rn"][:, 0:nt], u["nrm"][:, 0:nt], TINY, None, ALU.max))
                L.after(dve.reciprocal(u["rn"][:, 0:nt], u["rn"][:, 0:nt]))
                for tt in range(nt):
                    x1 = bu3[h][:, tt, 0:D]
                    a = dve.scalar_tensor_tensor(out=x1, in0=bu3[h][:, tt, D:2 * D], scalar=u["rn"][:, tt:tt + 1],
                                                 in1=x1, op0=ALU.mult, op1=ALU.add)
                a.then_inc(pair["x1_ready"][h], 1)
                dve.wait_ge(pair["x1_ready"][h], i + 1)
                for tt in range(nt):
                    a = dve.bn_stats(u["st"][:, tt, :], bu3[h][:, tt, 0:D])
                L.after(a)
                stand_alone(dve, s["waits_passed"])
                for tt in range(nt):
                    a = dve.bn_aggr(u["mv"][:, tt, :], u["st"][:, tt, :])
                L.after(a)
                dve.tensor_scalar(u["ve"][:, 0:nt], u["mv"][:, 0:nt, 1], EPS_LN, None, ALU.add).then_inc(pair["ve_ready"][h], 1)

            def r_h(i, h, t0, nt, rows):
                u = U[h]
                dve.wait_ge(pair["sdr"][h], i + 1)
                L.after(dve.reciprocal(u["rstd"][:, 0:nt], u["sd"][:, 0:nt]))
                for tt in range(nt):
                    a = dve.tensor_scalar(h3[h][:, tt, :], bu3[h][:, tt, 0:D], u["mv"][:, tt, 0:1], u["rstd"][:, tt:tt + 1],
                                          ALU.subtract, ALU.mult)
                a.then_inc(pair["h_ready"][h], 1)
                L.after(dve.tensor_tensor(u["t2"][:, 0:nt], u["mv"][:, 0:nt, 1], u["rstd"][:, 0:nt], ALU.mult))
                L.after(dve.tensor_tensor(u["t2"][:, 0:nt], u["t2"][:, 0:nt], u["rstd"][:, 0:nt], ALU.mult))
                dve.tensor_scalar(u["t2"][:, 0:nt], u["t2"][:, 0:nt], EPS_LN, None, ALU.add).then_inc(pair["t2_ready"][h], 1)

            def r_pick(i, h, t0, nt, rows):
                u = U[h]
                dve.wait_ge(pair["sd2r"][h], i + 1)
                until(dve, pair["scat"][h], 96 * i)
                L.after(dve.reciprocal(u["r2"][:, 0:nt], u["sd2"][:, 0:nt]))
                for tt in range(nt):
                    dve.tensor_scalar(pay[h][:, tt, 0:D], h3[h][:, tt, :], u["r2"][:, tt:tt + 1], None, ALU.mult)
                dve.wait_ge(pair["lg_mm"][h], i + 1)
                L.after(dve.tensor_tensor(u["lg"][:, 0:nt, :], bank[6 - 2 * h][:, 0:nt * 8].rearrange("p (t e) -> p t e", e=8),
                                          br_bc.rearrange("p (o e) -> p o e", o=1).to_broadcast([P, nt, 8]), ALU.add))
                stand_alone(dve, s["waits_passed"])
                for tt in range(nt):
                    a = dve.max(u["mx"][:, tt, :], u["lg"][:, tt, :])
                L.after(a)
                stand_alone(dve, s["waits_passed"])
                for tt in range(nt):
                    a = dve.max_index(u["ix"][:, tt, :].bitcast(U32), u["mx"][:, tt, :], u["lg"][:, tt, :])
                L.after(a)
                L.after(dve.tensor_copy(u["ixf"][:, 0:nt, :], u["ix"][:, 0:nt, 0:2].bitcast(U32)))
                i8 = iota8.rearrange("p (o e) -> p o e", o=1).to_broadcast([P, nt, 8])
                dve.tensor_tensor(u["oh1"][:, 0:nt, :], i8, u["ixf"][:, 0:nt, 0:1].to_broadcast([P, nt, 8]), ALU.is_equal)
                L.after(dve.tensor_tensor(u["oh2"][:, 0:nt, :], i8, u["ixf"][:, 0:nt, 1:2].to_broadcast([P, nt, 8]), ALU.is_equal))
                if rows < P:
                    L.after(dve.memset(u["M"][:, :, :], 0.0))
                dve.tensor_tensor(u["M"][0:rows, 0:nt, :], u["oh1"][0:rows, 0:nt, :], u["oh2"][0:rows, 0:nt, :], ALU.add)
                dve.tensor_tensor(u["dl"][:, 0:nt], u["mx"][:, 0:nt, 1], u["mx"][:, 0:nt, 0], ALU.subtract).then_inc(pair["pick_ready"][h], 1)

            def r_place(i, h, t0, nt, rows):
                u = U[h]
                dve.wait_ge(pair["e2_ready"][h], i + 1)
                L.after(dve.tensor_scalar(u["w1"][:, 0:nt], u["e2"][:, 0:nt], 1.0, None, ALU.add))
                L.after(dve.reciprocal(u["w1"][:, 0:nt], u["w1"][:, 0:nt]))
                L.after(dve.tensor_tensor(u["w2"][:, 0:nt], u["e2"][:, 0:nt], u["w1"][:, 0:nt], ALU.mult))

                def per_row(v):
                    return v[:, 0:nt].rearrange("p (t o) -> p t o", o=1).to_broadcast([P, nt, 8])
                dve.tensor_tensor(u["wv"][:, 0:nt, :], u["oh1"][:, 0:nt, :], per_row(u["w1"]), ALU.mult)
                L.after(dve.tensor_tensor(u["wt"][:, 0:nt, :], u["oh2"][:, 0:nt, :], per_row(u["w2"]), ALU.mult))
                dve.tensor_tensor(pay[h][:, 0:nt, W_AT:W_AT + EXPERTS], u["wv"][:, 0:nt, :], u["wt"][:, 0:nt, :], ALU.add)
                dve.tensor_copy(pay[h][:, 0:nt, ID_AT:ID_AT + 1], idcol[:, ds(t0, nt)].rearrange("p (t o) -> p t o", o=1))
                dve.wait_ge(pair["rank_mm"][h], i + 1)
                L.after(dve.tensor_tensor(u["rk"][:, 0:nt, :], bank[5][:, h * 32:h * 32 + nt * 8].rearrange("p (t e) -> p t e", e=8),
                                          eoff.rearrange("p (o e) -> p o e", o=1).to_broadcast([P, nt, 8]), ALU.add))
                for c, oh in enumerate(("oh1", "oh2")):
                    L.after(dve.tensor_tensor(u["pp"][:, 0:nt, :], u["rk"][:, 0:nt, :], u[oh][:, 0:nt, :], ALU.mult))
                    L.after(dve.tensor_reduce(u["posf"][:, 0:nt, c], u["pp"][:, 0:nt, :], AX, ALU.add))
                L.after(dve.tensor_reduce(u["dc"][:, :], u["M"][:, 0:nt, :].rearrange("p t e -> p e t"), AX, ALU.add))
                dve.tensor_copy(u["posi"].bitcast(I32)[:, 0:nt, :], u["posf"][:, 0:nt, :])
                dve.tensor_tensor(cnt[:, :], cnt[:, :], u["dc"][:, :], ALU.add).then_inc(pair["pay_ready"][h], 1)
                dve.wait_ge(pair["pay_ready"][h], i + 1)

            stages = (r_y, r_x1, r_h, r_pick, r_place)

            def route(i):
                for f in stages:
                    for h in range(2):
                        f(i, h, 6 * i + 3 * h, 3, P)
            repeat(dve, L, route, 0, UN)
            for f in stages:
                f(UN, 0, NT - 1, 1, TAIL)

            cf = U[1]["rk"][:, 0, :]
            ntf = U[1]["rk"][:, 1, :]
            ce = U[1]["rk"][:, 2, :]
            ci = U[1]["pp"][:, 0, :].bitcast(I32)
            dl8 = U[1]["pp"][:, 1, :]
            j8 = U[1]["pp"][:, 2, :]
            rc, ec = U[1]["ss"][:, 0:1], U[1]["ss"][:, 1:2]
            dve.wait_ge(s["mtab_cnt"], 1)
            L.after(dve.tensor_copy(cf, bank[5][:, 64:64 + EXPERTS]))
            dve.tensor_tensor(padpos_i, padpos, cf, ALU.add)
            L.after(dve.tensor_scalar(ci, cf, float(P - 1), None, ALU.add))
            L.after(dve.tensor_scalar(ci, ci, 7, None, ALU.logical_shift_right))
            L.after(dve.tensor_copy(ntf, ci))
            L.after(dve.tensor_tensor_scan(ce, ones49[:, 0:EXPERTS], ntf, 0.0, ALU.mult, ALU.add))
            L.after(dve.tensor_scalar(dl8, ntf, -float(P), float(CAP), ALU.mult, ALU.add))
            L.after(dve.scalar_tensor_tensor(out=j8, in0=ce, scalar=pcol, in1=dl8, op0=ALU.is_le, op1=ALU.mult, accum_out=rc))
            L.after(dve.scalar_tensor_tensor(out=j8, in0=ce, scalar=pcol, in1=ones49[:, 0:EXPERTS], op0=ALU.is_le, op1=ALU.mult, accum_out=ec))
            L.after(dve.scalar_tensor_tensor(out=rc, in0=pcol, scalar=float(P), in1=rc, op0=ALU.mult, op1=ALU.add))
            for h in range(2):
                dve.wait_ge(pair["scat"][h], 16 * (6 * UN + 2 * (1 - h)))
            posi = U[0]["posi"].bitcast(I32)
            dve.tensor_scalar(posi[:, 0, 0:1], rc, float(PADROW), None, ALU.min)
            dve.tensor_scalar(posi[:, 0, 1:2], ec, float(EXPERTS - 1), None, ALU.min)
            L.after(dve.memset(pay[1][:, 0, :], 0.0))
            dve.tensor_scalar(pay[1][:, 0, ID_AT:ID_AT + 1], pcol, float(NT * P), None, ALU.add).then_inc(s["mtab_ready"], 1)

            L.after(dve.memset(sel[:, :, :], 0.0))
            for e in range(EXPERTS):
                a = dve.tensor_scalar(sel[0:96, e, :], pm[0:96].to_broadcast([96, P]), float(e), None, ALU.is_equal)
            a.then_inc(s["sel_ready"], 1)

            dve.wait_ge(s["moetab_in"], 16)

            def copy_xeT(i, h):
                dve.wait_ge(pair["xeT_mm"][h], i + 1)
                until(dve, pair["h_mm"][h], 2 * i)
                until(dve, pair["ys_ready"][h], i)
                dve.tensor_copy(wid[h], xe[h][:, D:PAYW])
                dve.tensor_copy(xeT[h], bank[0][:, 0:D]).then_inc(pair["xeT_ready"][h], 1)

            def copy_hsT(i, h):
                dve.wait_ge(pair["hsT_mm"][h], 2 * i + 1)
                until(dve, pair["y_mm"][h], i)
                dve.tensor_copy(hsT[h][:, 0:512], bank[4][:, :]).then_inc(pair["hsT_dve"][h], 1)

            def weigh(i, h, e):
                dve.wait_ge(pair["y_mm"][h], i + 1)
                until(dve, pair["y_add"][h], 16 * i)
                dve.tensor_copy(nid[h], wid[h][:, ID_AT - D:ID_AT - D + 1])
                dve.tensor_scalar(ys[h], bank[6 + h][:, 0:D], wid[h][:, ds(W_AT - D + e, 1)], None, ALU.mult).then_inc(pair["ys_ready"][h], 1)
            copy_xeT(0, 0)

            def moe(i, last=False):
                es = [dve.value_load(moetab[0:1, ds(P + 2 * i + h, 1)], min_val=0, max_val=EXPERTS - 1) for h in range(2)]
                copy_xeT(i, 1)
                copy_hsT(i, 0)
                weigh(i, 0, es[0])
                if not last:
                    copy_xeT(i + 1, 0)
                copy_hsT(i, 1)
                weigh(i, 1, es[1])
            repeat(dve, None, moe, 0, MOE_TILES // 2 - 1)
            moe(MOE_TILES // 2 - 1, True)

        @block.tensor
        def _(pe):
            pe.wait_ge(s["consts_dve"], 3)

            def turn_unit(i, h, nt):
                pe.wait_ge(pair["xn_ready"][h], i + 1)
                for tt in range(nt):
                    if tt == 0:
                        if h == 1:
                            pe.wait_ge(pair["xnT_ready"][0], i + 1)
                        else:
                            until(pe, pair["xnT_ready"][1], i)
                    for c in range(DC):
                        m = pe.transpose(bank[tt][:, c * P:(c + 1) * P], xn[h][:, tt, c * P:(c + 1) * P], ident[:, :])
                    m.then_inc(pair["xnT_mm"][h], 1)

            def z_unit(i, h, nt):
                pe.wait_ge(pair["xnT_ready"][h], i + 1)
                if h == 1:
                    pe.wait_ge(pair["z_ready"][0], i + 1)
                else:
                    until(pe, pair["z_ready"][1], i)
                for tt in range(nt):
                    for c in range(DC):
                        m = pe.matmul(bank[3 + tt][:, 0:D], xnT[h][:, tt, c * P:(c + 1) * P], w_neigh[:, c, :],
                                      start=(c == 0), stop=(c == DC - 1))
                    m.then_inc(pair["z_mm"][h], 1)

            def ln_iter(i):
                for h in range(2):
                    turn_unit(i, h, 3)
                for h in range(2):
                    z_unit(i, h, 3)
            ln_iter(0)
            pe.wait_ge(s["cmp_ready"], 1)
            for k in range(2):
                for j in range(EJ):
                    m = pe.matmul(bank[6 + k][:, 0:NT], ones_b[0:EP, :], cmpb[0:EP, k * EJ + j, 0:NT], start=(j == 0), stop=(j == EJ - 1))
                m.then_inc(s["counts_ready"], 1)
            with pe.Fori(1, UN) as i:
                ln_iter(i)
            turn_unit(UN, 0, 1)
            z_unit(UN, 0, 1)
            pe.wait_ge(s["stepsf_ready"], 1)
            pe.wait_ge(pair["xnT_ready"][0], UN + 1)
            pe.wait_ge(pair["z_ready"][0], UN + 1)
            for k in range(2):
                for half, (j0, j1) in enumerate(((0, 4), (4, 7))):
                    for j in range(j0, j1):
                        m = pe.transpose(bank[2 * k + half][:, (j - j0) * P:(j - j0 + 1) * P], steps_f[:, j, k, :], ident[:, :])
                    m.then_inc(s["stepT_ready"], 1)
            pe.wait_ge(s["tables_ready"], 2)

            def walk(i, hooks={}):
                if -1 in hooks:
                    hooks[-1]()
                for k in range(STEP_BLOCK):
                    step = STEP_BLOCK * i + k
                    pe.wait_ge(g_in[k], 16 * (i + 1))
                    if k % S_GROUP == 0:
                        pe.wait_ge(s["s_built"], 2 * i + k // S_GROUP + 1)
                    if k % 2 == 0:
                        until(pe, s["acc_done"], PAIRS * (i - 1) + k // 2 + 1)
                    pe.matmul(bank[k // 2][:, 0:ACCW], S[:, k // S_GROUP, k % S_GROUP, :], G[:, k, :], start=(k % 2 == 0), stop=(k % 2 == 1)).then_inc(s["p_ready"], 1)
                    if k in hooks:
                        hooks[k]()

            def kv(t):
                pe.wait_ge(s["xa_in"], 16 * (t + 1))
                until(pe, s["kv_act"], t)
                for c in range(DC):
                    m = pe.matmul(bank[4][:, 0:2 * HID], xTs[:, c * P:(c + 1) * P], w_kv[:, c, :], start=(c == 0), stop=(c == DC - 1))
                m.then_inc(s["kv_mm"], 1)
            pe.wait_ge(s["consts_dve"], 4)
            repeat(pe, None, lambda i: walk(i, {6: lambda: kv(i)}), 0, NT - 1)
            kv(NT - 1)
            pe.wait_ge(s["kv_dve"], NT)
            pe.transpose(bank[6][:, 0:P], kmax, ident[:, :]).then_inc(s["kmaxT"], 1)
            pe.wait_ge(s["km_ready"], 1)
            pe.transpose(bank[6][:, 0:P], kmaxb, ident[:, :]).then_inc(s["kmaxrowT"], 1)
            pe.wait_ge(s["mk_exp"], 1)
            pe.matmul(bank[5][:, 0:HID + 2], mkT[:, :], mv1[:, :], start=True, stop=False, skip_group_check=True)

            def ctx_mm(g, nt=8, rows=P, last=False):
                pe.wait_ge(s["ek_exp"], g + 1)
                if isinstance(g, int):
                    pe.wait_ge(s["kv_act"], NT)
                for j in range(nt):
                    m = pe.matmul(bank[5][:, 0:HID + 2], ek[0:rows, j, :],
                                  kv_all[0:rows, ds(8 * g + j, 1), HID:KVW].rearrange("p o w -> p (o w)"),
                                  start=False, stop=last, skip_group_check=True)
                m.then_inc(s["ctx_mm"], 1)
            A2 = NT - 1
            repeat(pe, None, lambda i: walk(i, {7: lambda: ctx_mm(i - A2)}), A2, A2 + 6)
            ctx_mm(6, 1, TAIL, True)
            pe.wait_ge(s["ctx_ready"], 1)
            pe.transpose(bank[6][:, 0:P], ctxs, ident[:, :]).then_inc(s["ctxT_mm"], 1)
            pe.wait_ge(s["ctxT_ready"], 1)
            pe.matmul(bank[7][:, 0:D], ctxT, w_outs, start=True, stop=True).then_inc(s["M2_mm"], 1)
            pe.wait_ge(s["M2_ready"], 1)

            def qu(t):
                pe.wait_ge(s["xb_in"], 16 * (t + 1))
                until(pe, s["qu_evac"], t)
                for c in range(DC):
                    m = pe.matmul(bank[4][:, 0:HID + D], xTs[:, c * P:(c + 1) * P], w_qu[:, c, :], start=(c == 0), stop=(c == DC - 1))
                m.then_inc(s["qu_mm"], 1)

            def turn_q(t):
                pe.wait_ge(s["q_ready"], t + 1)
                pe.transpose(bank[6][:, 0:P], q_s, ident[:, :]).then_inc(s["qT_mm"], 1)

            def mix_out(t):
                pe.wait_ge(s["qT_sb"], t + 1)
                until(pe, s["o_evac"], t)
                pe.matmul(bank[7][:, 0:D], qT_s, M2[:, :], start=True, stop=True).then_inc(s["o_mm"], 1)

            def bfold(e, n):
                until(pe, s["bf_evac"], 2 * e + n)
                for c in range(DC):
                    m = pe.matmul(bank[5][0:EXPERTS, :], lnb[:, c, :], w1s[:, ds((e * DC + c) * HIDDEN + n * 512, 512)],
                                  start=(c == 0), stop=(c == DC - 1))
                m.then_inc(s["bf_mm"], 1)
            B0 = A2 + 6

            def b_hooks(t):
                return {-1: lambda: qu(t), 5: lambda: turn_q(t), 7: lambda: mix_out(t)}

            def fold_hooks(t):
                hk = b_hooks(t)
                e = t - 16
                hk[3] = lambda: bfold(e, 0)
                hk[6] = lambda: bfold(e, 1)
                return hk
            repeat(pe, None, lambda t: walk(t + B0, b_hooks(t)), 0, 16)
            pe.wait_ge(s["w1_in"], 16 * (EXPERTS + EXPERTS // 2))
            repeat(pe, None, lambda t: walk(t + B0, fold_hooks(t)), 16, 24)
            repeat(pe, None, lambda t: walk(t + B0, b_hooks(t)), 24, NT)
            for i in range(B0 + NT, BLOCKS):
                walk(i)
            pe.wait_ge(s["acc_done"], PAIRS * BLOCKS)

            def r_turn(i, h, nt):
                pe.wait_ge(pair["h_ready"][h], i + 1)
                until(pe, pair["hT_ready"][h], i)
                for tt in range(nt):
                    for c in range(DC):
                        m = pe.transpose(bank[2 * h + tt // 2][:, (tt % 2) * D + c * P:(tt % 2) * D + (c + 1) * P], h3[h][:, tt, c * P:(c + 1) * P], ident[:, :])
                m.then_inc(pair["hT_mm"][h], 1)

            def r_logits(i, h, nt):
                pe.wait_ge(pair["hT_ready"][h], i + 1)
                until(pe, pair["pick_ready"][h], i)
                for tt in range(nt):
                    for c in range(DC):
                        m = pe.matmul(bank[6 - 2 * h][:, tt * 8:tt * 8 + 8], hT3[h][:, tt, c * P:(c + 1) * P], Wr_s[:, c, :],
                                      start=(c == 0), stop=(c == DC - 1))
                m.then_inc(pair["lg_mm"][h], 1)

            def r_rank(i, h, nt):
                pe.wait_ge(pair["pick_ready"][h], i + 1)
                if h == 1:
                    pe.wait_ge(pair["pay_ready"][0], i + 1)
                else:
                    until(pe, pair["pay_ready"][1], i)
                M = U[h]["M"]
                for tt in range(nt):
                    to = bank[5][:, h * 32 + tt * 8:h * 32 + tt * 8 + 8]
                    pe.matmul(to, before[:, :], M[:, tt, :], start=True, stop=False)
                    for b in range(tt):
                        pe.matmul(to, ones_b[:, :], M[:, b, :], start=False, stop=False)
                    m = pe.matmul(to, ones_b[:, :], cnt[:, :], start=False, stop=True)
                m.then_inc(pair["rank_mm"][h], 1)

            def route(i):
                for f in (r_turn, r_logits, r_rank):
                    for h in range(2):
                        f(i, h, 3)
            repeat(pe, None, route, 0, UN)
            for f in (r_turn, r_logits, r_rank):
                f(UN, 0, 1)
            pe.wait_ge(pair["pay_ready"][0], UN + 1)
            pe.matmul(bank[5][:, 64:64 + EXPERTS], ones_b[:, :], cnt[:, :], start=True, stop=True).then_inc(s["mtab_cnt"], 1)

            pe.wait_ge(s["moetab_in"], 16)
            pe.wait_ge(s["sel_ready"], 1)
            pe.wait_ge(s["fold_done"], 2 * EXPERTS)

            def turn_x(i, h):
                pe.wait_ge(pair["xe_in"][h], 16 * (i + 1))
                if h == 1:
                    pe.wait_ge(pair["xeT_ready"][0], i + 1)
                else:
                    until(pe, pair["xeT_ready"][1], i)
                for c in range(DC):
                    m = pe.transpose(bank[0][:, c * P:(c + 1) * P], xe[h][:, c * P:(c + 1) * P], ident[:, :])
                m.then_inc(pair["xeT_mm"][h], 1)

            def layer1(i, h, e):
                pe.wait_ge(pair["xeT_ready"][h], i + 1)
                if h == 1:
                    pe.wait_ge(pair["gelu"][0], 2 * i + 2)
                else:
                    until(pe, pair["gelu"][1], 2 * i)
                for n in range(2):
                    to = bank[2 + n][:, :]
                    pe.matmul(to, sel[:, ds(e, 1), :].rearrange("p o n -> p (o n)"), brows[:, n * 512:(n + 1) * 512], start=True, stop=False)
                    for c in range(DC):
                        m = pe.matmul(to, xeT[h][:, c * P:(c + 1) * P], w1s[:, ds(e * (DC * HIDDEN) + c * HIDDEN + n * 512, 512)],
                                      start=False, stop=(c == DC - 1))
                    m.then_inc(pair["h_mm"][h], 1)

            def turn_h(i, h):
                for n in range(2):
                    pe.wait_ge(pair["gelu"][h], 2 * i + n + 1)
                    if n == 0:
                        other = pair["hsT_dve"], pair["hsT_act"]
                        if h == 1:
                            for o in other:
                                pe.wait_ge(o[0], i + 1)
                        else:
                            for o in other:
                                until(pe, o[1], i)
                    for c in range(4):
                        m = pe.transpose(bank[4 + n][:, c * P:(c + 1) * P], hs[h][:, (4 * n + c) * P:(4 * n + c + 1) * P], ident[:, :])
                    m.then_inc(pair["hsT_mm"][h], 1)

            def layer2(i, h, e):
                to = bank[6 + h][:, 0:D]
                until(pe, pair["ys_ready"][h], i)
                pe.matmul(to, sel[:, ds(e, 1), :].rearrange("p o n -> p (o n)"), brows[:, HIDDEN:HIDDEN + D], start=True, stop=False)
                for c in range(HC):
                    if c == 0:
                        pe.wait_ge(pair["hsT_dve"][h], i + 1)
                    if c == 4:
                        pe.wait_ge(pair["hsT_act"][h], i + 1)
                    m = pe.matmul(to, hsT[h][:, c * P:(c + 1) * P], w2s[:, ds(e * (HC * D) + c * D, D)], start=False, stop=(c == HC - 1))
                m.then_inc(pair["y_mm"][h], 1)

            def expert_of(k):
                return pe.value_load(moetab[0:1, ds(P + k, 1)], min_val=0, max_val=EXPERTS - 1)
            turn_x(0, 0)
            layer1(0, 0, expert_of(0))
            pe.wait_ge(s["late_in"], 16 * (EXPERTS // 2))

            def moe(i, last=False):
                e0, e1 = expert_of(2 * i), expert_of(2 * i + 1)
                turn_x(i, 1)
                turn_h(i, 0)
                layer1(i, 1, e1)
                layer2(i, 0, e0)
                if not last:
                    e2 = expert_of(2 * i + 2)
                    turn_x(i + 1, 0)
                turn_h(i, 1)
                if not last:
                    layer1(i + 1, 0, e2)
                layer2(i, 1, e1)
            repeat(pe, None, moe, 0, MOE_TILES // 2 - 1)
            moe(MOE_TILES // 2 - 1, True)


N_WEIGHTS = 21

_INS = ["x", "src", "dst", "L0_gnn_W", "L0_gnn_b", "L0_mix_w_qkv", "L0_mix_mem_kv", "L0_mix_w_out", "L0_mix_b_out",
        "L0_mix_g_out", "L0_mix_g_pre", "L0_ffn_Wr", "L0_ffn_br", "L0_ffn_ln_g", "L0_ffn_ln_b", "L0_ffn_W1",
        "L0_ffn_b1", "L0_ffn_W2", "L0_ffn_b2"]


def kernel(**inputs):
    import numpy as _np
    import concourse.bacc as _bacc
    from concourse import mybir as _mybir
    from concourse.bass_utils import run_bass_kernel_spmd as _run

    nc = _bacc.Bacc("TRN2", target_bir_lowering=False, num_devices=1)
    arrays, args = {}, []
    for name in _INS:
        a = _np.ascontiguousarray(inputs[name])
        arrays[f"in_{name}_dram"] = a
        args.append(nc.dram_tensor(f"in_{name}_dram", a.shape, _mybir.dt.from_np(a.dtype), kind="ExternalInput").ap())
    out = nc.dram_tensor("out_0_dram", (OUT_ROWS, D), F32, kind="ExternalOutput").ap()
    build_program(nc, *args, out)
    r = _run(nc, [arrays], core_ids=[0])
    return r.results[0]["out_0_dram"][0:N]
```

```python
from contextlib import ExitStack

import concourse.bass as bass
from concourse import mybir

F32 = mybir.dt.float32
BF16 = mybir.dt.bfloat16
F32R = mybir.dt.float32r
I32 = mybir.dt.int32
U32 = mybir.dt.uint32
ALU = mybir.AluOpType
ACT = mybir.ActivationFunctionType
AX = mybir.AxisListType.X
ds = bass.ds

P = 128
N = 6250
D = 256
DC = D // P
NT = (N + P - 1) // P
TAIL = N - (NT - 1) * P
EDGES = 100000
EROWS = 784
EFULL, EREST = EDGES // P, EDGES % P
EJ, EP = 7, EROWS // 7
NOWHERE = 1 << 20
STEPS_J = 7
STEP_BLOCK = 8
PAIRS = STEP_BLOCK // 2
S_GROUP = 4
TILE_BITS = 6
BLOCKS = (EFULL + 1 + (NT - 1) + NT + STEP_BLOCK - 1) // STEP_BLOCK
RT = 6
ACCW = D + 2
HEADS, HD = 4, 32
HID = HEADS * HD
MEM = 4
SPLITS = 4
KVW = 2 * HID + 2
EXPERTS, HIDDEN = 8, 1024
HC = HIDDEN // P
CAP = NT * P + P
PADROW = EXPERTS * CAP
PAYW = 266
W_AT, ID_AT = D, D + EXPERTS
MOE_TILES = 106
OUT_ROWS = NT * P + P
EPS_LN = 1e-5
TINY = 1e-12
SCALE = HD ** -0.5


class Links:

    def __init__(self, eng, sem):
        self.eng, self.sem, self.count = eng, sem, 0

    def after(self, ins):
        self.count = self.count + 1
        ins.then_inc(self.sem, 1)
        self.eng.wait_ge(self.sem, self.count)


def until(eng, sem, value):
    if isinstance(value, int) and value <= 0:
        return
    eng.wait_ge(sem, value)


def stand_alone(eng, passed):
    eng.sem_inc(passed, 1)


def repeat(eng, links, body, first, end):
    start = links.count if links else 0
    body(first)
    if end - first <= 1:
        return
    per = (links.count - start) if links else 0
    with eng.Fori(first + 1, end) as i:
        if links:
            links.count = start + (i - first) * per if per else start
        body(i)
    if links:
        links.count = start + (end - first) * per


def build_program(nc, x, src, dst, gnn_W, gnn_b, w_qkv, mem_kv, w_out, b_out, g_out, g_pre,
                  Wr, br, ln_g, ln_b, W1, b1, W2, b2, out):
    ctx = ExitStack()
    with ctx:
        def sb(name, shape, dt=F32):
            return ctx.enter_context(nc.sbuf_tensor(name, shape, dt))

        def shared(name, shape):
            with nc.sbuf_tensor(name + "_lent", shape, F32) as lent:
                pass
            return lent, sb(name, shape)

        def sem(name):
            return ctx.enter_context(nc.semaphore(name))

        def dram(name, shape, dt=F32):
            return nc.dram_tensor(name, shape, dt, kind="Internal").ap()

        edges_d = dram("edges_d", (EROWS, 2, P), I32)
        z_d = dram("z_d", (NT * P, D))
        xnT_d = dram("xnT_d", (NT, P, D))
        s_d = dram("s_d", (NT, P, D))
        bu_d = dram("bu_d", (NT, P, 2 * D))
        kept_d = dram("kept_d", (EROWS, 2, P), I32)
        step_d = dram("step_d", (P * STEPS_J,))
        bucket_d = dram("bucket_d", (PADROW + P, PAYW))
        w2hi_d = dram("w2hi_d", (EXPERTS, P, HC * D))
        w2lo_d = dram("w2lo_d", (EXPERTS, P, HC * D))
        moetab_d = dram("moetab_d", (2, P), I32)

        w1s = sb("w1s", [P, EXPERTS * DC * HIDDEN])
        w2s, w2s_r = shared("w2s", [P, EXPERTS * HC * D])
        taken = {"a": 0, "b": 0, "c": 0}
        LATE = EXPERTS * HC * D // 2

        def lend(stage, n):
            at = taken[stage]
            taken[stage] += n
            if stage != "a":
                assert at + n <= EXPERTS * HC * D - LATE
                return w2s[:, LATE + at:LATE + at + n]
            if at + n <= LATE:
                return w2s[:, at:at + n]
            at = max(at, LATE)
            taken[stage] = at + n
            at += NT * KVW - LATE
            assert at + n <= EXPERTS * DC * HIDDEN
            return w1s[:, at:at + n]

        x_all = w1s[:, 0:NT * D].rearrange("p (t d) -> p t d", d=D)
        kv_all = w1s[:, 0:NT * KVW].rearrange("p (t w) -> p t w", w=KVW)
        xn_flat = lend("a", 6 * D)
        xn = [xn_flat[:, 3 * D * h:3 * D * (h + 1)].rearrange("p (t d) -> p t d", d=D) for h in range(2)]
        xnT = [lend("a", 3 * D).rearrange("p (t d) -> p t d", d=D) for _ in range(2)]
        zs_flat = lend("a", 6 * D)
        zs = [zs_flat[:, 3 * D * h:3 * D * (h + 1)].rearrange("p (t d) -> p t d", d=D) for h in range(2)]
        ss = [lend("a", 3 * D).rearrange("p (t d) -> p t d", d=D) for _ in range(2)]
        w_neigh = lend("a", DC * D).rearrange("p (c d) -> p c d", c=DC)
        w_kv = lend("a", DC * 2 * HID).rearrange("p (c d) -> p c d", c=DC)
        headmask = lend("a", HID)
        w_outs = lend("a", D)
        mkT = lend("a", HID)[0:MEM]
        mv1 = lend("a", HID + 2)[0:MEM]
        thrL, thrF, Fr, cr, delta, pairs = (lend("a", NT) for _ in range(6))
        pairs = pairs.bitcast(I32)
        Lr = lend("a", NT + 1)
        firstlast = lend("a", 2 * EJ)
        ed_flat = lend("a", EJ * 2 * P)
        ed = ed_flat.bitcast(I32).rearrange("p (j k e) -> p j k e", j=EJ, k=2)
        steps_flat = lend("a", STEPS_J * 2 * P)
        steps_e = steps_flat.bitcast(I32).rearrange("p (j k e) -> p j k e", j=STEPS_J, k=2)
        epad = steps_flat[0:1, 0:2 * D].bitcast(I32)
        steps_f = ed_flat.rearrange("p (j k e) -> p j k e", j=STEPS_J, k=2)
        ek = zs_flat[:, 0:8 * HID].rearrange("p (t d) -> p t d", t=8)
        kmax, kmaxb, kmaxrow, ctxs, ctxT = (xn_flat[:, k * HID:(k + 1) * HID] for k in range(5))

        acc, acc_r = shared("acc", [P, NT + 1, ACCW])
        acc_flat = acc[:, :, :].rearrange("p t w -> p (t w)")
        edge_tabs, edge_tabs_r = shared("edge_tabs", [P, 2 * P * STEPS_J])
        srcT, dstT = edge_tabs[:, 0:P * STEPS_J].bitcast(I32), edge_tabs[:, P * STEPS_J:2 * P * STEPS_J]
        G = sb("G", [P, STEP_BLOCK, ACCW])
        S, S_r = shared("S", [P, 2, S_GROUP, P])
        S_flat = S[:, :, :, :].rearrange("p a b n -> p (a b n)")
        G_flat = G[:, :, :].rearrange("p k w -> p (k w)")
        junk = S_flat
        BUCKETS = NT + 1
        ones_f, before_f, hot, seen, base, ranks, cum = (S_flat[:, k * P:k * P + n] for k, n in enumerate(
            (P, P, BUCKETS, BUCKETS, BUCKETS, BUCKETS, BUCKETS)))
        sort1 = S_flat[:, 7 * P:8 * P]
        edge, at_i = sort1[:, 0:2].bitcast(I32), sort1[:, 2:4].bitcast(I32)
        tile_i, tile_f, pos_f, row_i, row_f, bad_f = (sort1[:, 4 + k:5 + k] for k in range(6))
        tile_i, row_i = tile_i.bitcast(I32), row_i.bitcast(I32)
        bad, bad_b, flag = sort1[:, 16:19], sort1[:, 20:22].bitcast(BF16), sort1[:, 24:25].bitcast(I32)
        next_first = sort1[:, 26:27].bitcast(I32)
        QW = HC * D // SPLITS
        w2raw, w2hi, w2lo = (w2s[:, k * QW:(k + 1) * QW] for k in range(3))
        w2_parts = W2.rearrange("e (q c p) n -> e q p c n", q=SPLITS, p=P)
        ident = sb("ident", [P, P])
        iota = sb("iota", [P, P])
        before = sb("before", [P, P], BF16)
        ones_b = sb("ones_b", [P, P], BF16)
        xTs = sb("xTs", [P, D])
        mean_rstd = sb("mean_rstd", [P, 2, 56])
        r16 = sb("r16", [P, NT])
        rdeg = sb("rdeg", [P, NT])
        brows = sb("brows", [P, D], BF16)
        b1T = sb("b1T", [P, EXPERTS * HC])
        small = sb("small", [P, 200])
        Wr_s = sb("Wr_s", [P, DC, EXPERTS])
        cnt = sb("cnt", [P, EXPERTS], BF16)
        used = [0]

        def tiny(n):
            used[0] += n
            assert used[0] <= 200
            return small[:, used[0] - n:used[0]]

        q_s = lend("b", HID)
        qT_s = lend("b", HID)
        o_s = lend("b", D)
        b_s = lend("b", D)
        u_s = lend("b", D)
        bacc = lend("b", HIDDEN)
        bres = lend("b", D)
        b2s = lend("b", D)
        w_qu = lend("b", DC * (HID + D)).rearrange("p (c n) -> p c n", c=DC)
        bg_bc, bo_bc, go_bc, M2, sB = (lend("b", D) for _ in range(5))
        drow_flat = lend("b", P * STEPS_J)[0:1, :]
        drow = drow_flat.rearrange("o (b k) -> o b k", k=STEP_BLOCK)
        packf = o_s[0:1, 0:P * STEPS_J // STEP_BLOCK]
        pack = drow_flat[:, 0:P * STEPS_J // STEP_BLOCK].bitcast(I32)
        cmpb = lend("b", 14 * 32).bitcast(BF16).rearrange("p (j d) -> p j d", j=14)
        sqj = lend("b", D)
        bsplit = lend("b", D // 2).bitcast(BF16)
        bu6 = [lend("c", RT * 2 * D).rearrange("p (t w) -> p t w", w=2 * D) for _ in range(2)]
        h6 = lend("c", RT * D).rearrange("p (t w) -> p t w", w=D)
        hT6 = G_flat[:, 0:RT * D].rearrange("p (t w) -> p t w", w=D)
        squares = S_flat.bitcast(BF16)[:, 0:RT * D].rearrange("p (t w) -> p t w", w=D)
        pay = edge_tabs[:, 0:RT * PAYW].rearrange("p (t w) -> p t w", w=PAYW)
        moe_at = [0]

        def inacc(n, flat=acc_flat):
            moe_at[0] += n
            assert moe_at[0] <= (NT + 1) * ACCW
            return flat[:, moe_at[0] - n:moe_at[0]]
        xe = [inacc(PAYW) for _ in range(2)]
        xeT = [inacc(D) for _ in range(2)]
        w1c = [inacc(DC * HIDDEN) for _ in range(2)]
        b1c = [inacc(HC) for _ in range(2)]
        hT = [G_flat[:, k * HIDDEN:(k + 1) * HIDDEN] for k in range(2)]
        ys = [inacc(D) for _ in range(2)]
        acc_r_flat = acc_r[:, :, :].rearrange("p t w -> p (t w)")
        w2l = [inacc(HC * D, acc_r_flat) for _ in range(2)]
        hhi = [inacc(HIDDEN, acc_r_flat) for _ in range(2)]
        hlo = [S_r[:, :, :, :].rearrange("p a b n -> p (a b n)"), edge_tabs_r[:, 0:HIDDEN]]
        wnext = [inacc(2) for _ in range(2)]
        wnow = [inacc(2) for _ in range(2)]
        nid = [inacc(2)[:, 0:1].bitcast(I32) for _ in range(2)]
        pay_last = xe[0].rearrange("p (o w) -> p o w", o=1)
        moetab = inacc(2 * P)[0:1, :].bitcast(I32)
        sel = inacc(EXPERTS * P // 2).bitcast(BF16).rearrange("p (e n) -> p e n", n=P)

        pcol = tiny(1)
        pm = tiny(1)
        gpre = tiny(DC)
        svals = tiny(STEPS_J)
        eoff = tiny(EXPERTS)
        iota8 = tiny(EXPERTS)
        padpos = tiny(EXPERTS)
        padpos_i = tiny(EXPERTS).bitcast(I32)
        idcol = tiny(NT)
        br_bc = tiny(EXPERTS)
        lng = tiny(EXPERTS * DC)
        lnb = tiny(EXPERTS * DC).rearrange("p (c e) -> p c e", c=DC)
        small2 = sb("small2", [P, 316])
        used2 = [0]

        def tiny2(n):
            used2[0] += n
            assert used2[0] <= 316
            return small2[:, used2[0] - n:used2[0]]
        cend = tiny2(NT)
        ecol = tiny2(STEPS_J)
        ecol_i = tiny2(STEPS_J).bitcast(I32)
        idx = [tiny2(STEP_BLOCK).bitcast(I32) for _ in range(2)]
        dcol = tiny2(STEPS_J)
        d128 = tiny2(STEPS_J)
        ones49 = tiny2(NT)
        var49 = tiny2(NT)
        t49 = tiny2(NT)
        bst6 = tiny2(6 * 6).rearrange("p (t s) -> p t s", s=6)
        mv6 = tiny2(6).rearrange("p (t k) -> p t k", k=2)
        kmem = tiny2(MEM)
        km1 = tiny2(1)
        km2 = tiny2(1)
        rS = tiny2(1)
        qm = tiny2(HEADS)
        qsum = tiny2(HEADS)
        rq = tiny2(HEADS)
        ssB = tiny2(1)
        nrmB = tiny2(1)
        rnB = tiny2(1)
        small3 = [xTs[:, :], edge_tabs[:, RT * PAYW:2 * P * STEPS_J]]
        used3 = [0, 0]

        def tiny3(*shape):
            n = 1
            for k in shape:
                n *= k
            k = 0 if used3[0] + n <= D else 1
            used3[k] += n
            assert used3[k] <= (D, 2 * P * STEPS_J - RT * PAYW)[k]
            v = small3[k][:, used3[k] - n:used3[k]]
            return v.rearrange("p (a b) -> p a b", b=shape[1]) if len(shape) == 2 else v
        rn, nrm, ss6, ve, sd, rstd6, t2, sd2, r2, dl, e2, w1, w2 = (tiny3(RT) for _ in range(13))
        st6, lg, mx, ix = tiny3(RT, 6), tiny3(RT, 8), tiny3(RT, 8), tiny3(RT, 8)
        mv, ixf, posf, posi_f = tiny3(RT, 2), tiny3(RT, 2), tiny3(RT, 2), tiny3(RT, 2)
        posi = posi_f.bitcast(I32)
        posi_last = tiny3(1, 2).bitcast(I32)
        tile_table = tiny3(2).bitcast(I32)
        padrow = G_flat[:, RT * D:RT * D + PAYW]
        small4 = sb("small4", [P, 6 * RT * EXPERTS])
        oh1, oh2, wv, wt, rk, pp = (small4[:, k * RT * EXPERTS:(k + 1) * RT * EXPERTS].rearrange("p (t e) -> p t e", e=EXPERTS)
                                    for k in range(6))
        picked = sb("picked", [P, RT, EXPERTS], BF16)
        dcnt = sb("dcnt", [P, EXPERTS])

        bank = [ctx.enter_context(nc.psum_tensor(f"bank{i}", [P, 512], F32)) for i in range(8)]

        names = """consts_pool consts_dve weights_in neigh_in dve_links act_links sort_links edges_written edges_in
            unsorted_mm unsorted_ready edges_kept row_in row_hot row_rank row_pos row_out bases_mm edges_in_again
            sd_ready rstd_ready sel_ready
            cmp_ready counts_ready ecol_ready step_rows_out drow_in steps_in stepsf_ready stepT_ready tables_ready
            s_built p_ready acc_done idx_ready waits_passed
            xa_in kv_mm kv_act kv_dve kmaxT km_ready kmaxrowT kmaxrow_ready mk_exp ek_sub ek_exp ctx_mm
            ctx_ready ctxT_mm ctxT_ready M2_mm M2_ready
            xb_in sb_in qu_mm qu_evac q_sub q_exp q_ready qT_mm qT_sb o_mm o_evac o_nrm bu_ready bu_out u_out
            w1_in w2raw_in w2_split w2_out bf_mm bf_evac fold_done b1_mm late_free w2_in
            y_ready nrm_ready ve_ready sd_done h_ready t2_ready sd2_done hT_mm hT_ready
            lg_mm pick_ready e2_ready rank_mm pay_ready scattered
            mtab_cnt mtab_ready mtab_out moetab_in zrows""".split()
        s = {n: sem(n) for n in names}
        pair = {n: [sem(f"{n}{h}") for h in range(2)] for n in (
            "x_in", "var_ready", "ln_sd", "xn_ready", "s_ready", "xnT_mm", "xnT_ready", "z_mm", "z_ready", "z_out", "xnT_out", "s_out",
            "bu_in", "x1_out",
            "xe_in", "xeT_mm", "xeT_ready", "w1c_ready", "h_mm", "gelu", "h_split", "w2l_in", "y_mm", "ys_ready", "y_add")}
        g_in = [sem(f"g_in{k}") for k in range(STEP_BLOCK)]

        UN = 8
        SCATTERED = 16 * 2 * NT
        x_t = x[0:(NT - 1) * P, :].rearrange("(t p) d -> p t d", p=P)
        z_t = z_d.rearrange("(t p) d -> p t d", p=P)
        xnT_t = xnT_d.rearrange("t p d -> p t d")
        s_t = s_d.rearrange("t p d -> p t d")
        bu_t = bu_d.rearrange("t p d -> p t d")
        out_t = out.rearrange("(t p) d -> p t d", p=P)

        def units(body_iter, eng, links):
            repeat(eng, links, body_iter, 0, UN)

        def load_w2(eng, first, end, done):
            for e in range(first, end):
                eng.dma_start(w2s_r[:, e * HC * D:(e + 1) * HC * D].bitcast(F32R), w2hi_d[e]).then_inc(done, 16)

        def split(eng, links, hi, lo, v):
            links.after(eng.tensor_copy(hi.bitcast(F32R), v))
            return eng.tensor_tensor(lo.bitcast(F32R), v, hi, ALU.subtract)

        SPLIT_AT = EXPERTS + 1
        SPLIT_END = SPLIT_AT + EXPERTS * SPLITS
        block = ctx.enter_context(nc.Block())

        @block.sync
        def _(sp):
            def load_x(i):
                for h in range(2):
                    until(sp, pair["x_in"][h], 16 * i)
                    sp.dma_start(x_all[:, ds(6 * i + 3 * h, 3), :], x_t[:, ds(6 * i + 3 * h, 3), :]).then_inc(pair["x_in"][h], 16)
            units(load_x, sp, None)
            sp.wait_ge(s["consts_dve"], 1)
            sp.wait_ge(pair["x_in"][0], 16 * UN)
            sp.dma_start(x_all[0:TAIL, NT - 1, :], x[(NT - 1) * P:N, :]).then_inc(pair["x_in"][0], 16)
            sp.wait_ge(s["ecol_ready"], 1)
            sp.dma_start(step_d.rearrange("(p j) -> p j", j=STEPS_J), dcol).then_inc(s["step_rows_out"], 16)
            sp.wait_ge(s["step_rows_out"], 16)
            sp.dma_start(drow, step_d.rearrange("(o b k) -> o b k", o=1, k=STEP_BLOCK)).then_inc(s["drow_in"], 16)

            def store_unit(i, h, t0, nt):
                sp.wait_ge(pair["s_ready"][h], i + 1)
                sp.dma_start(s_t[:, ds(t0, nt), :], ss[h][:, 0:nt, :]).then_inc(pair["s_out"][h], 16)
                sp.wait_ge(pair["xnT_ready"][h], i + 1)
                sp.dma_start(xnT_t[:, ds(t0, nt), :], xnT[h][:, 0:nt, :]).then_inc(pair["xnT_out"][h], 16)

            def store_z(i, h, t0, nt):
                sp.wait_ge(pair["z_ready"][h], i + 1)
                sp.dma_start(z_t[:, ds(t0, nt), :], zs[h][:, 0:nt, :]).then_inc(pair["z_out"][h], 16)

            def stores(i, first=False):
                store_unit(i, 0, 6 * i, 3)
                if not first:
                    store_z(i - 1, 1, 6 * i - 3, 3)
                store_unit(i, 1, 6 * i + 3, 3)
                store_z(i, 0, 6 * i, 3)
            stores(0, True)
            repeat(sp, None, stores, 1, UN)
            store_unit(UN, 0, NT - 1, 1)
            store_z(UN - 1, 1, NT - 4, 3)
            store_z(UN, 0, NT - 1, 1)
            for h in range(2):
                sp.wait_ge(pair["xnT_out"][h], 16 * (UN + 1 - h))
                sp.wait_ge(pair["s_out"][h], 16 * (UN + 1 - h))

            def load_a(t):
                until(sp, s["kv_mm"], t)
                sp.dma_start(xTs[:, :], xnT_d[ds(t, 1)].rearrange("o p d -> (o p) d")).then_inc(s["xa_in"], 16)
            repeat(sp, None, load_a, 0, NT - 1)
            load_a(NT - 1)
            sp.wait_ge(s["kv_mm"], NT)
            sp.dma_start(xTs[:, :], xnT_d[0]).then_inc(s["xb_in"], 16)
            sp.dma_start(sB[:, :], s_d[0]).then_inc(s["sb_in"], 16)

            def store_b(t):
                sp.wait_ge(s["bu_ready"], t + 1)
                sp.dma_start(bu_d[ds(t, 1), :, 0:D].rearrange("o p d -> (o p) d"), b_s).then_inc(s["bu_out"], 16)

            def io_b(t, first=False, last=False):
                if not last:
                    sp.wait_ge(s["qu_mm"], t + 1)
                    sp.dma_start(xTs[:, :], xnT_d[ds(t + 1, 1)].rearrange("o p d -> (o p) d")).then_inc(s["xb_in"], 16)
                sp.wait_ge(s["qu_evac"], t + 1)
                sp.dma_start(bu_d[ds(t, 1), :, D:2 * D].rearrange("o p d -> (o p) d"), u_s).then_inc(s["u_out"], 16)
                if not first:
                    store_b(t - 1)
                    sp.dma_start(sB[:, :], s_d[ds(t, 1)].rearrange("o p d -> (o p) d")).then_inc(s["sb_in"], 16)

            def io_load(t, to, frm):
                io_b(t)
                sp.dma_start(to, frm).then_inc(s["w1_in"], 16)

            def w1_of(e):
                return (w1s[:, ds(e * (DC * HIDDEN), DC * HIDDEN)].rearrange("p (c n) -> p c n", c=DC),
                        W1[ds(e, 1)].rearrange("o (c p) n -> p (o c) n", p=P))

            def store_split(e, q, n):
                sp.wait_ge(s["w2_split"], n + 1)
                for to, frm in ((w2hi_d, w2hi), (w2lo_d, w2lo)):
                    sp.dma_start(to[ds(e, 1), :, q * QW:(q + 1) * QW].rearrange("o p n -> (o p) n"), frm).then_inc(s["w2_out"], 16)

            def io_split(t, q):
                io_b(t)
                n = t - SPLIT_AT
                e = n - q * EXPERTS
                if not isinstance(t, int):
                    store_split(e - 1, q, n - 1)
                elif q > 0:
                    store_split(EXPERTS - 1, q - 1, n - 1)
                sp.dma_start(w2raw.rearrange("p (c n) -> p c n", n=D),
                             w2_parts[ds(e, 1), q].rearrange("o p c n -> p (o c) n")).then_inc(s["w2raw_in"], 16)
            io_b(0, first=True)
            sp.wait_ge(s["M2_ready"], 1)
            repeat(sp, None, lambda t: io_load(t, *w1_of(t - 1)), 1, SPLIT_AT)
            for q in range(SPLITS):
                repeat(sp, None, lambda t: io_split(t, q), SPLIT_AT + q * EXPERTS, SPLIT_AT + (q + 1) * EXPERTS)
            io_b(SPLIT_END)
            store_split(EXPERTS - 1, SPLITS - 1, EXPERTS * SPLITS - 1)
            repeat(sp, None, io_b, SPLIT_END + 1, NT - 1)
            io_b(NT - 1, last=True)
            store_b(NT - 1)
            sp.wait_ge(s["u_out"], 16 * NT)
            sp.wait_ge(s["bu_out"], 16 * NT)

            sp.wait_ge(s["late_free"], 1)

            def load_u(it, b, turn, nt):
                until(sp, pair["x1_out"][b], 16 * turn)
                sp.dma_start(bu6[b][:, 0:nt, :], bu_t[:, ds(RT * it, nt), :]).then_inc(pair["bu_in"][b], 16)

            def store_x1(it, b, nt):
                sp.wait_ge(s["h_ready"], 2 * it + (nt + 2) // 3)
                sp.dma_start(out_t[:, ds(RT * it, nt), :], bu6[b][:, 0:nt, 0:D]).then_inc(pair["x1_out"][b], 16)

            def route_io(turn, last=False):
                load_u(2 * turn + 1, 1, turn, RT)
                store_x1(2 * turn, 0, RT)
                load_u(2 * turn + 2, 0, turn + 1, 1 if last else RT)
                store_x1(2 * turn + 1, 1, RT)
            load_u(0, 0, 0, RT)
            sp.wait_ge(s["late_free"], 2)
            repeat(sp, None, route_io, 0, UN // 2 - 1)
            route_io(UN // 2 - 1, True)
            store_x1(UN, 0, 1)
            sp.wait_ge(s["mtab_ready"], 1)
            sp.dma_start(moetab_d.rearrange("k p -> p k"), tile_table,
                         allow_slow_non_contiguous=True).then_inc(s["mtab_out"], 16)
            sp.wait_ge(s["mtab_out"], 16)
            sp.dma_start(moetab[0:1, :], moetab_d.rearrange("(o k) p -> o (k p)", o=1)).then_inc(s["moetab_in"], 16)
            sp.wait_ge(s["zrows"], 16 * (EXPERTS + 2))
            sp.wait_ge(s["scattered"], SCATTERED)
            sp.wait_ge(s["moetab_in"], 16)

            def load_xe(i, h):
                r = sp.value_load(moetab[0:1, ds(2 * i + h, 1)], min_val=0, max_val=PADROW)
                until(sp, pair["xeT_ready"][h], i)
                sp.dma_start(xe[h][:, :], bucket_d[ds(r, P), :]).then_inc(pair["xe_in"][h], 16)

            load_xe(0, 0)
            load_xe(0, 1)

            def load_xes(i):
                for h in range(2):
                    load_xe(i, h)
            with sp.Fori(1, MOE_TILES // 2) as i:
                load_xes(i)
            for h in range(2):
                sp.wait_ge(pair["y_add"][h], 16 * (MOE_TILES // 2))

        @block.gpsimd
        def _(pool):
            def iota_f(ap, pattern, base, mult):
                return pool.iota(ap, pattern=pattern, base=base, channel_multiplier=mult, allow_small_or_imprecise_dtypes=True)
            iota_f(iota[:, :], [[1, P]], 0, 0)
            iota_f(pcol, [[0, 1]], 0, 1)
            iota_f(thrL, [[P, NT]], 0, 0)
            iota_f(thrF, [[P, NT]], P, 0)
            iota_f(svals, [[1, STEPS_J]], 0, STEPS_J)
            iota_f(eoff, [[CAP, EXPERTS]], 0, 0)
            iota_f(iota8, [[1, EXPERTS]], 0, 0)
            iota_f(padpos, [[CAP, EXPERTS]], 0, 1)
            iota_f(idcol, [[P, NT]], 0, 1).then_inc(s["consts_pool"], 1)
            pool.memset(acc_flat, 0.0).then_inc(s["consts_pool"], 1)

            def add_unit(i, h, t0, nt):
                pool.wait_ge(pair["xn_ready"][h], i + 1)
                until(pool, pair["s_out"][h], 16 * i)
                pool.tensor_tensor(ss[h][:, 0:nt, :], x_all[:, ds(t0, nt), :], xn[h][:, 0:nt, :], ALU.add).then_inc(pair["s_ready"][h], 1)

            def adds(i):
                for h in range(2):
                    add_unit(i, h, 6 * i + 3 * h, 3)
            def sort_places():
                pool.wait_ge(s["unsorted_ready"], 2)
                with pool.If(pool.value_load(flag[0:1, 0:1], min_val=0, max_val=1) > 0):
                    def place(row):
                        pool.wait_ge(s["row_pos"], row + 1)
                        stand_alone(pool, s["waits_passed"])
                        for k in range(2):
                            pool.indirect_dma_start(out=edges_d.rearrange("r k (e o) -> (r k e) o", o=1),
                                                    out_offset=bass.IndirectOffsetOnAxis(ap=at_i[:, k:k + 1], axis=0),
                                                    in_=edge[:, k:k + 1], in_offset=None).then_inc(s["row_out"], 16)
                    repeat(pool, None, place, 0, EROWS)
                    pool.wait_ge(s["row_out"], 32 * EROWS)

            def step_rows():
                pool.wait_ge(s["ecol_ready"], 1)
                for j in range(STEPS_J):
                    pool.indirect_dma_start(out=steps_e[:, j].rearrange("p k e -> p (k e)"), out_offset=None,
                                            in_=edges_d.rearrange("r k e -> r (k e)"),
                                            in_offset=bass.IndirectOffsetOnAxis(ap=ecol_i[:, j:j + 1], axis=0)
                                            ).then_inc(s["steps_in"], 16)
            adds(0)
            sort_places()
            step_rows()
            with pool.Fori(1, UN) as i:
                adds(i)
            add_unit(UN, 0, NT - 1, 1)

            pool.wait_ge(s["tables_ready"], 2)
            for h in range(2):
                pool.wait_ge(pair["z_out"][h], 16 * (UN + 1 - h))

            def copy_idx(b, half):
                pool.tensor_copy(idx[half], srcT[:, ds(STEP_BLOCK * b, STEP_BLOCK)]).then_inc(s["idx_ready"], 1)

            def gather_block(b, half, last=False):
                pool.wait_ge(s["idx_ready"], b + 1)
                for k in range(STEP_BLOCK):
                    until(pool, s["p_ready"], STEP_BLOCK * (b - 1) + k + 1)
                    if k == STEP_BLOCK - 1 and not last:
                        copy_idx(b + 1, 1 - half)
                    else:
                        stand_alone(pool, s["waits_passed"])
                    pool.indirect_dma_start(out=G[:, k, 0:D], out_offset=None, in_=z_d[:, :],
                                            in_offset=bass.IndirectOffsetOnAxis(ap=idx[half][:, k:k + 1], axis=0)
                                            ).then_inc(g_in[k], 16)
            copy_idx(0, 0)
            gather_block(0, 0)
            with pool.Fori(0, BLOCKS // 2 - 1) as i:
                gather_block(2 * i + 1, 1)
                gather_block(2 * i + 2, 0)
            gather_block(BLOCKS - 1, 1, True)

            pool.wait_ge(s["w2_out"], 32 * EXPERTS * SPLITS)
            load_w2(pool, 0, EXPERTS // 2, s["w2_in"])

            def scatters(it, nt=RT, rows=P, pay=pay, posi=posi):
                pool.wait_ge(s["pay_ready"], it + 1)
                stand_alone(pool, s["waits_passed"])
                for tt in range(nt):
                    for c in range(2):
                        pool.indirect_dma_start(out=bucket_d[:, :],
                                                out_offset=bass.IndirectOffsetOnAxis(ap=posi[0:rows, tt, c:c + 1], axis=0),
                                                in_=pay[0:rows, tt, :], in_offset=None).then_inc(s["scattered"], 16)
            pool.wait_ge(s["late_free"], 2)
            pool.dma_start(bucket_d[PADROW:PADROW + P, :], padrow).then_inc(s["zrows"], 16)
            pool.dma_start(out[NT * P:NT * P + P, :], padrow[:, 0:D]).then_inc(s["zrows"], 16)
            repeat(pool, None, scatters, 0, UN)
            scatters(UN, 1, TAIL, pay_last, posi_last)
            pool.wait_ge(s["mtab_ready"], 1)
            for e in range(EXPERTS):
                pool.indirect_dma_start(out=bucket_d[:, :], out_offset=bass.IndirectOffsetOnAxis(ap=padpos_i[:, e:e + 1], axis=0),
                                        in_=padrow, in_offset=None).then_inc(s["zrows"], 16)
            for h in range(2):
                pool.wait_ge(pair["x1_out"][h], 16 * (UN // 2 + 1 - h))
            pool.wait_ge(s["pay_ready"], UN + 1)
            load_w2(pool, EXPERTS // 2, EXPERTS, s["w2_in"])
            pool.wait_ge(s["zrows"], 16 * (EXPERTS + 2))

            def load_w2l(i, h):
                e = pool.value_load(moetab[0:1, ds(P + 2 * i + h, 1)], min_val=0, max_val=EXPERTS - 1)
                if not isinstance(i, int) or i > 0:
                    pool.wait_ge(pair["y_mm"][h], i)
                    stand_alone(pool, s["waits_passed"])
                pool.dma_start(w2l[h].bitcast(F32R), w2lo_d[ds(e, 1)].rearrange("o p n -> (o p) n")).then_inc(pair["w2l_in"][h], 16)
            pool.wait_ge(s["moetab_in"], 16)
            for h in range(2):
                load_w2l(0, h)

            def add_y(i, h):
                pool.wait_ge(pair["ys_ready"][h], i + 1)
                until(pool, pair["y_add"][1 - h], 16 * (i + h))
                stand_alone(pool, s["waits_passed"])
                pool.indirect_dma_start(out=out[:, :], out_offset=bass.IndirectOffsetOnAxis(ap=nid[h], axis=0),
                                        in_=ys[h], in_offset=None, compute_op=ALU.add).then_inc(pair["y_add"][h], 16)

            def adds_y(i, last=False):
                for h in range(2):
                    if not last:
                        load_w2l(i + 1, h)
                    add_y(i, h)
            repeat(pool, None, adds_y, 0, MOE_TILES // 2 - 1)
            adds_y(MOE_TILES // 2 - 1, True)

        @block.scalar
        def _(act):
            L = Links(act, s["act_links"])
            w = s["edges_written"]
            act.dma_start(edges_d[0:EFULL, 0, :], src[0:EFULL * P].rearrange("(r e) -> r e", e=P)).then_inc(w, 16)
            act.dma_start(edges_d[0:EFULL, 1, :], dst[0:EFULL * P].rearrange("(r e) -> r e", e=P)).then_inc(w, 16)
            act.dma_start(edges_d[EFULL:EFULL + 1, 0, 0:EREST], src[EFULL * P:EDGES].rearrange("(r e) -> r e", r=1)).then_inc(w, 16)
            act.dma_start(edges_d[EFULL:EFULL + 1, 1, 0:EREST], dst[EFULL * P:EDGES].rearrange("(r e) -> r e", r=1)).then_inc(w, 16)
            act.wait_ge(s["consts_dve"], 1)
            nr = EROWS - EFULL - 1
            act.dma_start(edges_d[EFULL:EFULL + 1, 0, EREST:P], epad[0:1, 0:P - EREST]).then_inc(w, 16)
            act.dma_start(edges_d[EFULL:EFULL + 1, 1, EREST:P], epad[0:1, D:D + P - EREST]).then_inc(w, 16)
            act.dma_start(edges_d[EFULL + 1:EROWS, 0, :], epad[0:1, 0:nr * P].rearrange("p (r e) -> p r e", e=P)).then_inc(w, 16)
            act.dma_start(edges_d[EFULL + 1:EROWS, 1, :], epad[0:1, D:D + nr * P].rearrange("p (r e) -> p r e", e=P)).then_inc(w, 16)
            act.wait_ge(w, 8 * 16)
            act.dma_start(ed[0:EP], edges_d.rearrange("(p j) k e -> p j k e", j=EJ)).then_inc(s["edges_in"], 16)
            act.dma_start(next_first[0:EP - 1], edges_d.rearrange("(p j) k e -> p j k e", j=EJ)[1:EP, 0, 1, 0:1],
                          allow_slow_non_contiguous=True).then_inc(s["edges_in"], 16)
            act.dma_start(w_neigh, gnn_W[D:2 * D, :].rearrange("(c p) n -> p c n", p=P)).then_inc(s["neigh_in"], 16)

            def unit_sd(i, h, t0, nt):
                act.wait_ge(pair["var_ready"][h], i + 1)
                sd = mean_rstd[:, 1, ds(t0, nt)]
                act.activation(sd, sd, ACT.Sqrt).then_inc(pair["ln_sd"][h], 1)

            def copy_xnT(i, h, nt):
                act.wait_ge(pair["xnT_mm"][h], i + 1)
                until(act, pair["xnT_out"][h], 16 * i)
                until(act, pair["z_mm"][h], i)
                if nt > 2:
                    act.activation(xnT[h][:, 2, :], bank[2 * h + 1][:, 0:D], ACT.Copy)
                n = min(nt, 2)
                act.activation(xnT[h][:, 0:n, :], bank[2 * h][:, 0:n * D].rearrange("p (t d) -> p t d", d=D),
                               ACT.Copy).then_inc(pair["xnT_ready"][h], 1)

            def copies(i):
                for h in range(2):
                    copy_xnT(i, h, 3)
                    unit_sd(i + 1, h, 6 * i + 6 + 3 * h, 3)
            for h in range(2):
                unit_sd(0, h, 3 * h, 3)
            copies(0)
            n_w = 0
            for to, frm in ((w_qu[:, :, HID:HID + D], gnn_W[0:D, :].rearrange("(c p) n -> p c n", p=P)),
                            (w_qu[:, :, 0:HID], w_qkv[:, 0:HID].rearrange("(c p) n -> p c n", p=P)),
                            (w_kv, w_qkv[:, HID:3 * HID].rearrange("(c p) n -> p c n", p=P)),
                            (bg_bc[:, :], gnn_b.rearrange("(o d) -> o d", o=1).to_broadcast([P, D])),
                            (bo_bc[:, :], b_out.rearrange("(o d) -> o d", o=1).to_broadcast([P, D])),
                            (go_bc[:, :], g_out.rearrange("(o d) -> o d", o=1).to_broadcast([P, D])),
                            (br_bc, br.rearrange("(o d) -> o d", o=1).to_broadcast([P, EXPERTS])),
                            (w_outs, w_out[:, :]),
                            (kmem, mem_kv[0].rearrange("h d m -> (h d) m")),
                            (Wr_s[:, :, :], Wr.rearrange("(c p) n -> p c n", p=P)),
                            (bacc[0:EXPERTS, :], b1[:, :]),
                            (b2s[0:EXPERTS, :], b2[:, :])):
                act.dma_start(to, frm).then_inc(s["weights_in"], 16)
                n_w += 1
            with nc.allow_non_contiguous_dma(reason="small parameters, transposed once"):
                for c in range(DC):
                    act.dma_start(gpre[:, c:c + 1], g_pre[c * P:(c + 1) * P].rearrange("(p o) -> p o", o=1)).then_inc(s["weights_in"], 16)
                    act.dma_start(lng.rearrange("p (e c) -> p e c", c=DC)[:, :, c:c + 1],
                                  ln_g[:, c * P:(c + 1) * P].rearrange("e (p o) -> p e o", o=1)).then_inc(s["weights_in"], 16)
                    act.dma_start(lnb[:, c, :], ln_b[:, c * P:(c + 1) * P].rearrange("e p -> p e")).then_inc(s["weights_in"], 16)
                act.dma_start(mkT[:, :], mem_kv[0].rearrange("h d m -> m (h d)")).then_inc(s["weights_in"], 16)
                act.dma_start(mv1[:, 0:HID], mem_kv[1].rearrange("h d m -> m (h d)")).then_inc(s["weights_in"], 16)
            assert n_w + 3 * DC + 2 == N_WEIGHTS
            act.wait_ge(s["unsorted_ready"], 2)
            with act.If(act.value_load(flag[0:1, 0:1], min_val=0, max_val=1) > 0):
                act.dma_start(kept_d, edges_d).then_inc(s["edges_kept"], 16)
                act.wait_ge(s["edges_kept"], 16)

                def feed(row):
                    until(act, s["row_out"], 32 * row)
                    with nc.allow_non_contiguous_dma(reason="one edge per partition"):
                        act.dma_start(edge, kept_d[ds(row, 1)].rearrange("o k e -> e (o k)")).then_inc(s["row_in"], 16)
                repeat(act, None, feed, 0, EROWS)
                act.wait_ge(s["row_out"], 32 * EROWS)
                act.dma_start(ed[0:EP], edges_d.rearrange("(p j) k e -> p j k e", j=EJ)).then_inc(s["edges_in_again"], 16)
            repeat(act, None, copies, 1, UN - 1)
            copy_xnT(UN - 1, 0, 3)
            unit_sd(UN, 0, NT - 1, 1)
            copy_xnT(UN - 1, 1, 3)
            copy_xnT(UN, 0, 1)
            act.wait_ge(s["rstd_ready"], 1)
            act.activation(r16[:, :], t49, ACT.Sqrt).then_inc(s["sd_ready"], 1)

            def kv(t):
                act.wait_ge(s["kv_mm"], t + 1)
                act.activation(kv_all[:, ds(t, 1), 0:2 * HID].rearrange("p o w -> p (o w)"), bank[4][:, 0:2 * HID], ACT.Copy,
                               scale=r16[:, ds(t, 1)]).then_inc(s["kv_act"], 1)
            act.wait_ge(s["rstd_ready"], 2)
            repeat(act, None, kv, 0, NT - 1)
            kv(NT - 1)
            act.wait_ge(s["kmaxrow_ready"], 1)
            act.activation(mkT[:, :], mkT[:, :], ACT.Exp).then_inc(s["mk_exp"], 1)

            def exp_k(g, nt=8, rows=P):
                act.wait_ge(s["ek_sub"], g + 1)
                act.activation(ek[0:rows, 0:nt, :], ek[0:rows, 0:nt, :], ACT.Exp).then_inc(s["ek_exp"], 1)
            repeat(act, None, exp_k, 0, 6)
            exp_k(6, 1, TAIL)

            def exp_q(t):
                act.wait_ge(s["q_sub"], t + 1)
                act.activation(q_s, q_s, ACT.Exp).then_inc(s["q_exp"], 1)

            def norm_o(t):
                act.wait_ge(s["o_evac"], t + 1)
                L.after(act.activation(sqj, o_s, ACT.Square, accum_out=ssB))
                act.activation(nrmB, ssB, ACT.Sqrt).then_inc(s["o_nrm"], 1)

            def copy_qT(t):
                act.wait_ge(s["qT_mm"], t + 1)
                until(act, s["o_mm"], t)
                act.activation(qT_s, bank[6][:, 0:P], ACT.Copy).then_inc(s["qT_sb"], 1)

            def mix(t):
                exp_q(t)
                norm_o(t - 1)
                copy_qT(t)

            def mix_and_fold(t):
                mix(t)
                j = t - 24
                if isinstance(t, int):
                    act.wait_ge(s["bf_mm"], 2 * EXPERTS)
                w = w1s[:, ds(j * HIDDEN, HIDDEN)]
                act.activation(w, w, ACT.Copy, scale=lng[:, ds(j, 1)]).then_inc(s["fold_done"], 1)
            exp_q(0)
            copy_qT(0)
            repeat(act, L, mix, 1, 24)
            repeat(act, L, mix_and_fold, 24, 40)
            repeat(act, L, mix, 40, NT)
            norm_o(NT - 1)

            def r_relu(it, b, nt=RT):
                for first in range(0, nt, 3):
                    act.wait_ge(s["y_ready"], 2 * it + first // 3 + 1)
                    y = bu6[b][:, first:min(first + 3, nt), D:2 * D]
                    a = act.activation(y, y, ACT.Relu)
                L.after(a)
                for tt in range(nt):
                    a = act.activation(squares[:, tt, :], bu6[b][:, tt, D:2 * D], ACT.Square, accum_out=ss6[:, tt:tt + 1])
                L.after(a)
                act.activation(nrm[:, 0:nt], ss6[:, 0:nt], ACT.Sqrt).then_inc(s["nrm_ready"], 1)

            def r_sd(it, nt):
                act.wait_ge(s["ve_ready"], it + 1)
                act.activation(sd[:, 0:nt], ve[:, 0:nt], ACT.Sqrt).then_inc(s["sd_done"], 1)
                act.wait_ge(s["t2_ready"], it + 1)
                act.activation(sd2[:, 0:nt], t2[:, 0:nt], ACT.Sqrt).then_inc(s["sd2_done"], 1)

            def r_hT(it, nt):
                for half in range((nt + 2) // 3):
                    act.wait_ge(s["hT_mm"], 2 * it + half + 1)
                    left = min(nt - 3 * half, 3)
                    if left > 2:
                        act.activation(hT6[:, 3 * half + 2, :], bank[2 * half + 1][:, 0:D], ACT.Copy)
                    n = min(left, 2)
                    act.activation(hT6[:, 3 * half:3 * half + n, :], bank[2 * half][:, 0:n * D].rearrange("p (t d) -> p t d", d=D),
                                   ACT.Copy).then_inc(s["hT_ready"], 1)

            def r_e2(it, nt):
                act.wait_ge(s["pick_ready"], it + 1)
                act.activation(e2[:, 0:nt], dl[:, 0:nt], ACT.Exp).then_inc(s["e2_ready"], 1)

            def route(turn, last=False):
                for b in range(2):
                    it = 2 * turn + b
                    r_sd(it, RT)
                    r_hT(it, RT)
                    r_relu(it + 1, 1 - b, 1 if last and b else RT)
                    r_e2(it, RT)
            r_relu(0, 0)
            repeat(act, L, route, 0, UN // 2 - 1)
            route(UN // 2 - 1, True)
            r_sd(UN, 1)
            r_hT(UN, 1)
            r_e2(UN, 1)
            def gelu(i, h):
                for c in range(HC):
                    if c % 4 == 0:
                        act.wait_ge(pair["h_mm"][h], 2 * i + c // 4 + 1)
                    if c == 0:
                        until(act, pair["y_mm"][h], i)
                    a = act.activation(hT[h][:, c * P:(c + 1) * P], bank[2 * h + c // 4][:, (c % 4) * P:(c % 4 + 1) * P], ACT.Gelu,
                                       bias=b1c[h][:, c:c + 1])
                    if c % 4 == 3:
                        a.then_inc(pair["gelu"][h], 1)

            def gelus(i):
                for h in range(2):
                    gelu(i, h)
            repeat(act, None, gelus, 0, MOE_TILES // 2)

        @block.vector
        def _(dve):
            L = Links(dve, s["dve_links"])
            dve.memset(epad[0:1, 0:D], 0)
            dve.memset(epad[0:1, D:2 * D], NOWHERE)
            dve.memset(x_all[:, NT - 1, :], 0.0).then_inc(s["consts_dve"], 1)
            dve.memset(G[:, :, D:ACCW], 1.0)
            dve.memset(ones_b[:, :], 1.0)
            dve.memset(ones49, 1.0)
            dve.memset(cnt[:, :], 0.0)
            dve.memset(brows[:, :], 0.0)
            dve.memset(mv1[:, HID:HID + 2], 1.0)
            dve.memset(headmask, 0.0)
            L.after(dve.memset(delta[:, NT - 1:NT], float(EROWS)))
            for hd in range(HEADS):
                a = dve.memset(headmask[hd * HD:(hd + 1) * HD, hd * HD:(hd + 1) * HD], SCALE)
            L.after(a)
            dve.wait_ge(s["consts_pool"], 1)
            dve.tensor_scalar(ident[:, :], iota[:, :], pcol, None, ALU.is_equal).then_inc(s["consts_dve"], 1)
            dve.tensor_scalar(before[:, :], iota[:, :], pcol, None, ALU.is_gt)
            for k in range(3):
                a = dve.tensor_scalar(pm[32 * k:32 * k + 32], pcol[32 * k:32 * k + 32], -32.0 * k, None, ALU.add)
            L.after(a)

            def stats(i, h, t0, nt):
                dve.wait_ge(pair["x_in"][h], 16 * (i + 1))
                for tt in range(nt):
                    a = dve.bn_stats(bst6[:, tt, :], x_all[:, ds(t0 + tt, 1), :].rearrange("p o d -> p (o d)"))
                L.after(a)
                stand_alone(dve, s["waits_passed"])
                for tt in range(nt):
                    a = dve.bn_aggr(mv6[:, tt, :], bst6[:, tt, :])
                L.after(a)
                dve.tensor_copy(mean_rstd[:, 0, ds(t0, nt)], mv6[:, 0:nt, 0])
                dve.tensor_copy(var49[:, ds(t0, nt)], mv6[:, 0:nt, 1])
                dve.tensor_scalar(mean_rstd[:, 1, ds(t0, nt)], mv6[:, 0:nt, 1], EPS_LN, None, ALU.add).then_inc(pair["var_ready"][h], 1)

            def norm_unit(i, h, t0, nt):
                dve.wait_ge(pair["ln_sd"][h], i + 1)
                rstd = mean_rstd[:, 1, ds(t0, nt)]
                L.after(dve.reciprocal(rstd, rstd))
                until(dve, pair["xnT_mm"][h], i)
                until(dve, pair["s_ready"][h], i)
                for tt in range(nt):
                    a = dve.tensor_scalar(xn[h][:, tt, :], x_all[:, ds(t0 + tt, 1), :].rearrange("p o d -> p (o d)"),
                                          mean_rstd[:, 0, ds(t0 + tt, 1)], mean_rstd[:, 1, ds(t0 + tt, 1)],
                                          ALU.subtract, ALU.mult)
                a.then_inc(pair["xn_ready"][h], 1)

            def z_unit(i, h, nt):
                dve.wait_ge(pair["z_mm"][h], i + 1)
                until(dve, pair["z_out"][h], 16 * i)
                if nt > 2:
                    dve.tensor_copy(zs[h][:, 2, :], bank[5 + 2 * h][:, 0:D])
                n = min(nt, 2)
                dve.tensor_copy(zs[h][:, 0:n, :], bank[4 + 2 * h][:, 0:n * D].rearrange("p (t d) -> p t d", d=D)
                                ).then_inc(pair["z_ready"][h], 1)

            def norm_iter(i, first=False, last=False):
                norm_unit(i, 0, 6 * i, 3)
                stats(i + 1, 0, 6 * i + 6, 1 if last else 3)
                if not first:
                    z_unit(i - 1, 0, 3)
                norm_unit(i, 1, 6 * i + 3, 3)
                if not last:
                    stats(i + 1, 1, 6 * i + 9, 3)
                if not first:
                    z_unit(i - 1, 1, 3)

            def sort_check():
                dve.wait_ge(s["edges_in"], 32)
                dst_of = ed[0:EP, :, 1, :]
                dve.memset(bad, 0.0)
                L.after(dve.memset(bad_b, 0.0))
                n = EJ * (P - 1)
                gt = steps_flat[0:EP, 0:n].rearrange("p (j e) -> p j e", e=P - 1)
                dve.tensor_tensor(gt, dst_of[:, :, 0:P - 1], dst_of[:, :, 1:P], ALU.is_gt)
                gt_rows = steps_flat[0:EP, n:n + EJ - 1].rearrange("p (j e) -> p j e", e=1)
                dve.tensor_tensor(gt_rows, dst_of[:, 0:EJ - 1, P - 1:P], dst_of[:, 1:EJ, 0:1], ALU.is_gt)
                L.after(dve.tensor_tensor(bad[0:EP - 1, 1:2], dst_of[0:EP - 1, EJ - 1, P - 1:P], next_first[0:EP - 1], ALU.is_gt))
                L.after(dve.tensor_reduce(bad[0:EP, 0:1], steps_flat[0:EP, 0:n + EJ - 1], AX, ALU.max))
                dve.tensor_tensor(bad_b[:, 0:1], bad[:, 0:1], bad[:, 1:2], ALU.max).then_inc(s["unsorted_ready"], 1)
                dve.wait_ge(s["unsorted_mm"], 1)
                dve.tensor_scalar(flag, bank[6][:, 0:1], 1.0, None, ALU.min).then_inc(s["unsorted_ready"], 1)
                dve.wait_ge(s["unsorted_ready"], 2)

            def sort_edges():
                SL = Links(dve, s["sort_links"])
                dve.memset(ones_f, 1.0)
                dve.tensor_copy(before_f, before[:, :])
                dve.memset(seen, 0.0)
                tiles_i = steps_flat[0:EP, 0:EJ * P].bitcast(I32)
                tiles = steps_flat[0:EP, EJ * P:2 * EJ * P]
                SL.after(dve.tensor_copy(tiles_i.rearrange("p (j e) -> p j e", e=P), ed[0:EP, :, 1, :]))
                SL.after(dve.tensor_scalar(tiles_i, tiles_i, 7, None, ALU.logical_shift_right))
                SL.after(dve.tensor_scalar(tiles, tiles_i, float(NT), None, ALU.min))
                SL.after(dve.memset(hot, 0.0))

                def count(b):
                    SL.after(dve.tensor_scalar(steps_flat[0:EP, 0:EJ * P], tiles, iota[0:EP, ds(b, 1)], None, ALU.is_equal))
                    SL.after(dve.tensor_reduce(hot[0:EP, ds(b, 1)], steps_flat[0:EP, 0:EJ * P], AX, ALU.add))
                repeat(dve, SL, count, 0, BUCKETS)
                dve.sem_inc(s["bases_mm"], 1)
                dve.wait_ge(s["bases_mm"], 2)
                SL.after(dve.tensor_copy(ranks, bank[6][:, 0:BUCKETS]))
                SL.after(dve.tensor_tensor_scan(cum, ones_f[:, 0:BUCKETS], ranks, 0.0, ALU.mult, ALU.add))
                SL.after(dve.tensor_tensor(base, cum, ranks, ALU.subtract))

                def sort_row(row):
                    dve.wait_ge(s["row_in"], 16 * (row + 1))
                    SL.after(dve.tensor_scalar(tile_i, edge[:, 1:2], 7, None, ALU.logical_shift_right))
                    SL.after(dve.tensor_scalar(tile_f, tile_i, float(NT), None, ALU.min))
                    dve.tensor_scalar(hot, iota[:, 0:BUCKETS], tile_f, None, ALU.is_equal).then_inc(s["row_hot"], 1)
                    dve.wait_ge(s["row_rank"], row + 1)
                    SL.after(dve.tensor_tensor(ranks, bank[6][:, 0:BUCKETS], base, ALU.add))
                    SL.after(dve.tensor_tensor(ranks, ranks, hot, ALU.mult))
                    dve.tensor_tensor(seen, seen, hot, ALU.add)
                    SL.after(dve.tensor_reduce(pos_f, ranks, AX, ALU.add))
                    SL.after(dve.tensor_copy(row_i, pos_f))
                    SL.after(dve.tensor_scalar(row_i, row_i, 7, None, ALU.logical_shift_right))
                    SL.after(dve.tensor_copy(row_f, row_i))
                    SL.after(dve.scalar_tensor_tensor(out=pos_f, in0=row_f, scalar=float(P), in1=pos_f, op0=ALU.mult, op1=ALU.add))
                    dve.tensor_copy(at_i[:, 0:1], pos_f)
                    dve.tensor_scalar(at_i[:, 1:2], pos_f, float(P), None, ALU.add).then_inc(s["row_pos"], 1)
                repeat(dve, SL, sort_row, 0, EROWS)
                dve.wait_ge(s["edges_in_again"], 16)

            def step_tables():
                sort_check()
                with dve.If(dve.value_load(flag[0:1, 0:1], min_val=0, max_val=1) > 0):
                    sort_edges()
                tables()

            def tables():
                fl = firstlast.rearrange("p (k j) -> p k j", k=2)
                dve.tensor_copy(fl[0:EP, 0, :], ed[0:EP, :, 1, P - 1:P].rearrange("p j o -> p (j o)"))
                L.after(dve.tensor_copy(fl[0:EP, 1, :], ed[0:EP, :, 1, 0:1].rearrange("p j o -> p (j o)")))
                for k, thr in ((0, thrL), (1, thrF)):
                    for j in range(EJ):
                        a = dve.tensor_scalar(cmpb[0:EP, k * EJ + j, 0:NT], thr[0:EP], fl[0:EP, k, j:j + 1], None, ALU.is_gt)
                a.then_inc(s["cmp_ready"], 1)
                dve.wait_ge(s["counts_ready"], 2)
                dve.tensor_copy(Lr[:, 0:NT], bank[6][:, 0:NT])
                L.after(dve.tensor_copy(Fr, bank[7][:, 0:NT]))
                L.after(dve.tensor_tensor(cr, Fr, Lr[:, 0:NT], ALU.subtract))
                L.after(dve.tensor_scalar(pairs, cr, 1.0, None, ALU.add))
                L.after(dve.tensor_scalar(pairs, pairs, 1, None, ALU.logical_shift_right))
                L.after(dve.tensor_scalar(cr, pairs, 2.0, None, ALU.mult))
                L.after(dve.tensor_tensor_scan(cend, ones49, cr, 0.0, ALU.mult, ALU.add))
                L.after(dve.tensor_tensor(Fr, Lr[:, 0:NT], cr, ALU.add))
                L.after(dve.tensor_tensor(delta[:, 0:NT - 1], Lr[:, 1:NT], Fr[:, 0:NT - 1], ALU.subtract))
                for j in range(STEPS_J):
                    for k, (per_tile, col) in enumerate(((delta, ecol), (ones49, dcol))):
                        at = (2 * j + k) * NT
                        a = dve.scalar_tensor_tensor(out=junk[:, at:at + NT], in0=cend, scalar=svals[:, j:j + 1], in1=per_tile,
                                                     op0=ALU.is_le, op1=ALU.mult, accum_out=col[:, j:j + 1])
                L.after(a)
                L.after(dve.tensor_tensor(ecol, ecol, svals, ALU.add))
                dve.tensor_scalar(ecol_i, ecol, float(EROWS - 1), None, ALU.min)
                dve.tensor_scalar(d128, dcol, float(P), None, ALU.mult).then_inc(s["ecol_ready"], 1)
            for h in range(2):
                stats(0, h, 3 * h, 3)
            norm_iter(0, first=True)
            step_tables()
            norm_iter(1)
            dve.wait_ge(s["weights_in"], 16 * N_WEIGHTS)
            for c in range(DC):
                dve.tensor_scalar(w_kv[:, c, :], w_kv[:, c, :], gpre[:, c:c + 1], None, ALU.mult)
                dve.tensor_scalar(w_qu[:, c, 0:HID], w_qu[:, c, 0:HID], gpre[:, c:c + 1], None, ALU.mult)
            dve.tensor_scalar(go_bc[:, :], go_bc[:, :], float(D) ** 0.5, None, ALU.mult).then_inc(s["consts_dve"], 1)
            repeat(dve, L, norm_iter, 2, UN - 1)
            norm_iter(UN - 1, last=True)
            norm_unit(UN, 0, NT - 1, 1)
            z_unit(UN - 1, 0, 3)
            dve.wait_ge(s["steps_in"], 16 * STEPS_J)
            dve.wait_ge(s["ecol_ready"], 1)
            dve.tensor_copy(steps_f[:, :, 0, :], steps_e[:, :, 0, :])
            for j in range(STEPS_J):
                a = dve.tensor_scalar(steps_f[:, j, 1, :], steps_e[:, j, 1, :], d128[:, j:j + 1], None, ALU.subtract)
            a.then_inc(s["stepsf_ready"], 1)
            z_unit(UN - 1, 1, 3)
            for k, tab in ((0, srcT), (1, dstT)):
                to = tab[:, :].rearrange("e (p j) -> e j p", j=STEPS_J)
                for half, (j0, j1) in enumerate(((0, 4), (4, 7))):
                    dve.wait_ge(s["stepT_ready"], 2 * k + half + 1)
                    a = dve.tensor_copy(to[:, j0:j1, :], bank[2 * k + half][:, 0:(j1 - j0) * P].rearrange("e (j p) -> e j p", p=P))
                a.then_inc(s["tables_ready"], 1)
            z_unit(UN, 0, 1)
            rstd = mean_rstd[:, 1, 0:NT]
            L.after(dve.tensor_tensor(t49, var49, rstd, ALU.mult))
            L.after(dve.tensor_tensor(t49, t49, rstd, ALU.mult))
            dve.tensor_scalar(t49, t49, float(D), None, ALU.mult).then_inc(s["rstd_ready"], 1)
            dve.wait_ge(s["sd_ready"], 1)
            L.after(dve.tensor_scalar(r16[:, :], r16[:, :], TINY, None, ALU.max))
            L.after(dve.reciprocal(r16[:, :], r16[:, :]))
            dve.tensor_scalar(r16[:, :], r16[:, :], float(D) ** 0.5, None, ALU.mult).then_inc(s["rstd_ready"], 1)
            dve.wait_ge(s["tables_ready"], 2)
            dve.wait_ge(s["rstd_ready"], 2)
            for h in range(2):
                dve.wait_ge(pair["s_ready"][h], UN + 1 - h)
            dve.memset(kmax, -3e38)
            dve.memset(kv_all[:, :, 2 * HID:KVW], 1.0).then_inc(s["consts_dve"], 1)
            dve.wait_ge(s["drow_in"], 16)

            def pair_tile(k):
                return drow[:, :, 2 * k:2 * k + 1].rearrange("o b k -> o (b k)")
            L.after(dve.scalar_tensor_tensor(out=packf, in0=pair_tile(PAIRS - 1), scalar=float(1 << TILE_BITS),
                                             in1=pair_tile(PAIRS - 2), op0=ALU.mult, op1=ALU.add))
            for k in range(PAIRS - 3, -1, -1):
                L.after(dve.scalar_tensor_tensor(out=packf, in0=packf, scalar=float(1 << TILE_BITS), in1=pair_tile(k),
                                                 op0=ALU.mult, op1=ALU.add))
            L.after(dve.tensor_copy(pack, packf))

            def build_S(group, slot):
                dve.tensor_tensor(S[:, slot, :, :], iota[:, :].rearrange("p (o n) -> p o n", o=1).to_broadcast([P, S_GROUP, P]),
                                  dstT[:, ds(S_GROUP * group, S_GROUP)].rearrange("p (g o) -> p g o", o=1).to_broadcast([P, S_GROUP, P]),
                                  ALU.is_equal).then_inc(s["s_built"], 1)

            def walk(i, hooks={}):
                word = dve.value_load(pack[0:1, ds(i, 1)])
                for k in range(STEP_BLOCK):
                    step = STEP_BLOCK * i + k
                    if k % S_GROUP == 0:
                        until(dve, s["p_ready"], step)
                        build_S(2 * i + k // S_GROUP + 1, (k // S_GROUP + 1) % 2)
                    if k % 2:
                        pair_no = PAIRS * i + k // 2
                        dve.wait_ge(s["p_ready"], step + 1)
                        until(dve, s["acc_done"], pair_no)
                        tile = (word >> (TILE_BITS * (k // 2))) & ((1 << TILE_BITS) - 1)
                        tile = nc.s_assert_within(tile, 0, NT, skip_runtime_bounds_check_because="a count of at most NT tiles")
                        to = acc_flat[:, ds(tile * ACCW, ACCW)]
                        dve.tensor_tensor(to, to, bank[k // 2][:, 0:ACCW], ALU.add).then_inc(s["acc_done"], 1)
                    if k in hooks:
                        hooks[k]()
            build_S(0, 0)
            dve.wait_ge(s["consts_pool"], 2)

            def kmax_tile(t, rows=P):
                dve.wait_ge(s["kv_act"], t + 1)
                until(dve, s["kv_dve"], t)
                dve.tensor_tensor(kmax[0:rows], kv_all[0:rows, ds(t, 1), 0:HID].rearrange("p o w -> p (o w)"), kmax[0:rows],
                                  ALU.max).then_inc(s["kv_dve"], 1)
            repeat(dve, L, lambda i: walk(i, {7: lambda: kmax_tile(i)}), 0, NT - 1)
            kmax_tile(NT - 1, TAIL)
            dve.wait_ge(s["kmaxT"], 1)
            dve.tensor_reduce(km1, bank[6][:, 0:P], AX, ALU.max)
            L.after(dve.tensor_reduce(km2, kmem, AX, ALU.max))
            L.after(dve.tensor_tensor(km1, km1, km2, ALU.max))
            dve.tensor_copy(kmaxb, km1.to_broadcast([P, HID])).then_inc(s["km_ready"], 1)
            dve.wait_ge(s["kmaxrowT"], 1)
            L.after(dve.tensor_copy(kmaxrow, bank[6][:, 0:P]))
            dve.tensor_tensor(mkT[:, :], mkT[:, :], kmaxrow[0:MEM], ALU.subtract).then_inc(s["kmaxrow_ready"], 1)

            def sub_k(g, nt=8, rows=P):
                until(dve, s["ctx_mm"], g + 0)
                dve.wait_ge(s["kv_act"], NT)
                dve.tensor_tensor(ek[0:rows, 0:nt, :], kv_all[0:rows, ds(8 * g, nt), 0:HID],
                                  kmaxrow[0:rows].rearrange("p (o d) -> p o d", o=1).to_broadcast([rows, nt, HID]),
                                  ALU.subtract).then_inc(s["ek_sub"], 1)
            A2 = NT - 1
            repeat(dve, L, lambda i: walk(i, {0: lambda: sub_k(i - A2)}), A2, A2 + 6)
            sub_k(6, 1, TAIL)
            dve.wait_ge(s["ctx_mm"], 7)
            L.after(dve.reciprocal(rS, bank[5][:, HID:HID + 1]))
            dve.scalar_tensor_tensor(out=ctxs, in0=bank[5][:, 0:HID], scalar=rS, in1=headmask,
                                     op0=ALU.mult, op1=ALU.mult).then_inc(s["ctx_ready"], 1)
            dve.wait_ge(s["ctxT_mm"], 1)
            dve.tensor_copy(ctxT, bank[6][:, 0:P]).then_inc(s["ctxT_ready"], 1)
            dve.wait_ge(s["M2_mm"], 1)
            dve.tensor_copy(M2[:, :], bank[7][:, 0:D]).then_inc(s["M2_ready"], 1)

            q4 = q_s.rearrange("p (h d) -> p h d", h=HEADS)

            def heads(v):
                return v.rearrange("p (h o) -> p h o", o=1).to_broadcast([P, HEADS, HD])

            def b_q1(t):
                dve.wait_ge(s["qu_mm"], t + 1)
                L.after(dve.tensor_scalar(q_s, bank[4][:, 0:HID], r16[:, ds(t, 1)], None, ALU.mult))
                L.after(dve.tensor_reduce(qm, q4, AX, ALU.max))
                dve.tensor_tensor(q4, q4, heads(qm), ALU.subtract).then_inc(s["q_sub"], 1)
                until(dve, s["u_out"], 16 * t)
                dve.tensor_tensor(u_s, bank[4][:, HID:HID + D], bg_bc[:, :], ALU.add).then_inc(s["qu_evac"], 1)

            def b_q2(t):
                dve.wait_ge(s["q_exp"], t + 1)
                L.after(dve.tensor_reduce(qsum, q4, AX, ALU.add))
                L.after(dve.reciprocal(rq, qsum))
                dve.tensor_tensor(q4, q4, heads(rq), ALU.mult).then_inc(s["q_ready"], 1)

            def b_o1(t):
                dve.wait_ge(s["o_mm"], t + 1)
                dve.tensor_tensor(o_s, bank[7][:, 0:D], bo_bc[:, :], ALU.add).then_inc(s["o_evac"], 1)

            def b_o2(t):
                dve.wait_ge(s["o_nrm"], t + 1)
                dve.wait_ge(s["sb_in"], 16 * (t + 1))
                until(dve, s["bu_out"], 16 * t)
                L.after(dve.tensor_scalar(rnB, nrmB, TINY, None, ALU.max))
                L.after(dve.reciprocal(rnB, rnB))
                L.after(dve.scalar_tensor_tensor(out=o_s, in0=o_s, scalar=rnB, in1=go_bc[:, :], op0=ALU.mult, op1=ALU.mult))
                dve.tensor_tensor(b_s, o_s, sB[:, :], ALU.add).then_inc(s["bu_ready"], 1)

            B0 = A2 + 6

            def b_hooks(t, first=False):
                hk = {0: lambda: b_q1(t), 3: lambda: b_q2(t)}
                if not first:
                    hk[1] = lambda: b_o1(t - 1)
                    hk[6] = lambda: b_o2(t - 1)
                return hk

            def b_fold(e, n):
                dve.wait_ge(s["bf_mm"], 2 * e + n + 1)
                c = bacc[0:EXPERTS, n * 512:(n + 1) * 512]
                dve.scalar_tensor_tensor(out=c, in0=bank[5][0:EXPERTS, :], scalar=ident[0:EXPERTS, ds(e, 1)],
                                         in1=c, op0=ALU.mult, op1=ALU.add).then_inc(s["bf_evac"], 1)

            def with_split(hooks):
                def more(t):
                    n = t - SPLIT_AT - 1

                    def split_w2():
                        dve.wait_ge(s["w2raw_in"], 16 * (n + 1))
                        until(dve, s["w2_out"], 32 * n)
                        split(dve, L, w2hi, w2lo, w2raw).then_inc(s["w2_split"], 1)
                    return {**hooks(t), 5: split_w2}
                return more

            def fold_hooks(t):
                hk = b_hooks(t)
                e = t - 16
                hk[4] = lambda: (until(dve, s["bf_evac"], 2 * e), b_fold(e, 0))
                hk[7] = lambda: b_fold(e, 1)
                return hk
            walk(B0, b_hooks(0, True))
            for first, end, hooks in ((1, SPLIT_AT + 1, b_hooks), (SPLIT_AT + 1, 16, with_split(b_hooks)), (16, 24, with_split(fold_hooks)),
                                      (24, SPLIT_END + 1, with_split(b_hooks)), (SPLIT_END + 1, NT, b_hooks)):
                repeat(dve, L, lambda t: walk(t + B0, hooks(t)), first, end)
            walk(B0 + NT, {1: lambda: b_o1(NT - 1), 6: lambda: b_o2(NT - 1)})
            dve.wait_ge(s["b1_mm"], 1)
            dve.tensor_copy(b1T[:, :].rearrange("p (e c) -> p c e", c=HC), bank[5][:, 0:HC * EXPERTS].rearrange("p (c e) -> p c e", e=EXPERTS))
            L.after(dve.tensor_copy(bres[0:EXPERTS, :], b2s[0:EXPERTS, :]))
            for k in range(3):
                to = brows[32 * k:32 * k + EXPERTS, :]
                L.after(dve.tensor_copy(brows[0:EXPERTS, :] if k == 0 else bsplit[0:EXPERTS, :], bres[0:EXPERTS, :]))
                part = brows[0:EXPERTS, :] if k == 0 else bsplit[0:EXPERTS, :]
                if k:
                    dve.tensor_copy(to, part)
                if k < 2:
                    L.after(dve.tensor_tensor(bres[0:EXPERTS, :], bres[0:EXPERTS, :], part, ALU.subtract))
            dve.wait_ge(s["bu_out"], 16 * NT)
            dve.memset(picked[:, :, :], 0.0).then_inc(s["late_free"], 1)
            repeat(dve, L, walk, B0 + NT + 1, BLOCKS)
            dve.wait_ge(s["acc_done"], PAIRS * BLOCKS)
            deg = acc[:, 0:NT, D:D + 1].rearrange("p t o -> p (t o)")
            L.after(dve.tensor_scalar(rdeg[:, :], deg, 1.0, None, ALU.max))
            L.after(dve.reciprocal(rdeg[:, :], rdeg[:, :]))
            for tt in range(RT):
                dve.memset(pay[:, tt, ID_AT:PAYW], 0.0)
            L.after(dve.memset(padrow, 0.0))
            dve.tensor_scalar(padrow[:, ID_AT:ID_AT + 1], pcol, float(NT * P), None, ALU.add).then_inc(s["late_free"], 1)

            def r_y(it, b, turn, nt=RT):
                dve.wait_ge(pair["bu_in"][b], 16 * (turn + 1))
                for tt in range(nt):
                    y = bu6[b][:, tt, D:2 * D]
                    a = dve.scalar_tensor_tensor(out=y, in0=acc[:, ds(RT * it + tt, 1), 0:D].rearrange("p o d -> p (o d)"),
                                                 scalar=rdeg[:, ds(RT * it + tt, 1)], in1=y, op0=ALU.mult, op1=ALU.add)
                    if tt % 3 == 2 or tt == nt - 1:
                        a.then_inc(s["y_ready"], 1)

            def r_x1(it, b, nt):
                dve.wait_ge(s["nrm_ready"], it + 1)
                L.after(dve.tensor_scalar(rn[:, 0:nt], nrm[:, 0:nt], TINY, None, ALU.max))
                L.after(dve.reciprocal(rn[:, 0:nt], rn[:, 0:nt]))
                for tt in range(nt):
                    x1 = bu6[b][:, tt, 0:D]
                    a = dve.scalar_tensor_tensor(out=x1, in0=bu6[b][:, tt, D:2 * D], scalar=rn[:, tt:tt + 1],
                                                 in1=x1, op0=ALU.mult, op1=ALU.add)
                L.after(a)
                for tt in range(nt):
                    a = dve.bn_stats(st6[:, tt, :], bu6[b][:, tt, 0:D])
                L.after(a)
                stand_alone(dve, s["waits_passed"])
                for tt in range(nt):
                    a = dve.bn_aggr(mv[:, tt, :], st6[:, tt, :])
                L.after(a)
                dve.tensor_scalar(ve[:, 0:nt], mv[:, 0:nt, 1], EPS_LN, None, ALU.add).then_inc(s["ve_ready"], 1)

            def r_h(it, b, nt):
                dve.wait_ge(s["sd_done"], it + 1)
                L.after(dve.reciprocal(rstd6[:, 0:nt], sd[:, 0:nt]))
                for tt in range(nt):
                    a = dve.tensor_scalar(h6[:, tt, :], bu6[b][:, tt, 0:D], mv[:, tt, 0:1], rstd6[:, tt:tt + 1],
                                          ALU.subtract, ALU.mult)
                    if tt % 3 == 2 or tt == nt - 1:
                        a.then_inc(s["h_ready"], 1)
                L.after(dve.tensor_tensor(t2[:, 0:nt], mv[:, 0:nt, 1], rstd6[:, 0:nt], ALU.mult))
                L.after(dve.tensor_tensor(t2[:, 0:nt], t2[:, 0:nt], rstd6[:, 0:nt], ALU.mult))
                dve.tensor_scalar(t2[:, 0:nt], t2[:, 0:nt], EPS_LN, None, ALU.add).then_inc(s["t2_ready"], 1)

            def r_pick(it, nt, rows):
                dve.wait_ge(s["lg_mm"], it + 1)
                L.after(dve.tensor_tensor(lg[:, 0:nt, :], bank[6][:, 0:nt * EXPERTS].rearrange("p (t e) -> p t e", e=EXPERTS),
                                          br_bc.rearrange("p (o e) -> p o e", o=1).to_broadcast([P, nt, EXPERTS]), ALU.add))
                stand_alone(dve, s["waits_passed"])
                for tt in range(nt):
                    a = dve.max(mx[:, tt, :], lg[:, tt, :])
                L.after(a)
                stand_alone(dve, s["waits_passed"])
                for tt in range(nt):
                    a = dve.max_index(ix[:, tt, :].bitcast(U32), mx[:, tt, :], lg[:, tt, :])
                L.after(a)
                L.after(dve.tensor_copy(ixf[:, 0:nt, :], ix[:, 0:nt, 0:2].bitcast(U32)))
                i8 = iota8.rearrange("p (o e) -> p o e", o=1).to_broadcast([P, nt, EXPERTS])
                dve.tensor_tensor(oh1[:, 0:nt, :], i8, ixf[:, 0:nt, 0:1].to_broadcast([P, nt, EXPERTS]), ALU.is_equal)
                L.after(dve.tensor_tensor(oh2[:, 0:nt, :], i8, ixf[:, 0:nt, 1:2].to_broadcast([P, nt, EXPERTS]), ALU.is_equal))
                if rows < P:
                    L.after(dve.memset(picked[:, :, :], 0.0))
                dve.tensor_tensor(picked[0:rows, 0:nt, :], oh1[0:rows, 0:nt, :], oh2[0:rows, 0:nt, :], ALU.add)
                dve.tensor_tensor(dl[:, 0:nt], mx[:, 0:nt, 1], mx[:, 0:nt, 0], ALU.subtract).then_inc(s["pick_ready"], 1)

            def r_place(it, nt, pay=pay, posi=posi):
                dve.wait_ge(s["sd2_done"], it + 1)
                if nt == RT:
                    until(dve, s["scattered"], 16 * 2 * RT * it)
                else:
                    dve.memset(pay[:, 0, ID_AT:PAYW], 0.0)
                L.after(dve.reciprocal(r2[:, 0:nt], sd2[:, 0:nt]))
                for tt in range(nt):
                    dve.tensor_scalar(pay[:, tt, 0:D], h6[:, tt, :], r2[:, tt:tt + 1], None, ALU.mult)
                dve.tensor_copy(pay[:, 0:nt, ID_AT:ID_AT + 1], idcol[:, ds(RT * it, nt)].rearrange("p (t o) -> p t o", o=1))
                dve.tensor_reduce(dcnt[:, :], picked[:, 0:nt, :].rearrange("p t e -> p e t"), AX, ALU.add)
                dve.wait_ge(s["rank_mm"], it + 1)
                L.after(dve.tensor_tensor(rk[:, 0:nt, :], bank[5][:, 0:nt * EXPERTS].rearrange("p (t e) -> p t e", e=EXPERTS),
                                          eoff.rearrange("p (o e) -> p o e", o=1).to_broadcast([P, nt, EXPERTS]), ALU.add))
                dve.tensor_tensor(wv[:, 0:nt, :], rk[:, 0:nt, :], oh1[:, 0:nt, :], ALU.mult)
                L.after(dve.tensor_tensor(pp[:, 0:nt, :], rk[:, 0:nt, :], oh2[:, 0:nt, :], ALU.mult))
                dve.tensor_reduce(posf[:, 0:nt, 0], wv[:, 0:nt, :], AX, ALU.add)
                L.after(dve.tensor_reduce(posf[:, 0:nt, 1], pp[:, 0:nt, :], AX, ALU.add))
                dve.tensor_copy(posi[:, 0:nt, :], posf[:, 0:nt, :])
                dve.tensor_tensor(cnt[:, :], cnt[:, :], dcnt[:, :], ALU.add)
                dve.wait_ge(s["e2_ready"], it + 1)
                L.after(dve.tensor_scalar(w1[:, 0:nt], e2[:, 0:nt], 1.0, None, ALU.add))
                L.after(dve.reciprocal(w1[:, 0:nt], w1[:, 0:nt]))
                L.after(dve.tensor_tensor(w2[:, 0:nt], e2[:, 0:nt], w1[:, 0:nt], ALU.mult))

                def per_row(v):
                    return v[:, 0:nt].rearrange("p (t o) -> p t o", o=1).to_broadcast([P, nt, EXPERTS])
                dve.tensor_tensor(wv[:, 0:nt, :], oh1[:, 0:nt, :], per_row(w1), ALU.mult)
                L.after(dve.tensor_tensor(wt[:, 0:nt, :], oh2[:, 0:nt, :], per_row(w2), ALU.mult))
                dve.tensor_tensor(pay[:, 0:nt, W_AT:W_AT + EXPERTS], wv[:, 0:nt, :], wt[:, 0:nt, :], ALU.add).then_inc(s["pay_ready"], 1)
                dve.wait_ge(s["pay_ready"], it + 1)

            def route(turn, last=False):
                for b in range(2):
                    it = 2 * turn + b
                    r_x1(it, b, RT)
                    r_h(it, b, RT)
                    r_y(it + 1, 1 - b, turn + b, 1 if last and b else RT)
                    r_pick(it, RT, P)
                    r_place(it, RT)
            r_y(0, 0, 0)
            repeat(dve, L, route, 0, UN // 2 - 1)
            route(UN // 2 - 1, True)
            r_x1(UN, 0, 1)
            r_h(UN, 0, 1)
            r_pick(UN, 1, TAIL)
            r_place(UN, 1, pay_last, posi_last)

            cf, ntf, ce = (rk[:, k, :] for k in range(3))
            ci, dl8, j8 = pp[:, 0, :].bitcast(I32), pp[:, 1, :], pp[:, 2, :]
            rc, ec = ss6[:, 0:1], ss6[:, 1:2]
            dve.wait_ge(s["mtab_cnt"], 1)
            L.after(dve.tensor_copy(cf, bank[5][:, 64:64 + EXPERTS]))
            dve.tensor_tensor(padpos_i, padpos, cf, ALU.add)
            L.after(dve.tensor_scalar(ci, cf, float(P - 1), None, ALU.add))
            L.after(dve.tensor_scalar(ci, ci, 7, None, ALU.logical_shift_right))
            L.after(dve.tensor_copy(ntf, ci))
            L.after(dve.tensor_tensor_scan(ce, ones49[:, 0:EXPERTS], ntf, 0.0, ALU.mult, ALU.add))
            L.after(dve.tensor_scalar(dl8, ntf, -float(P), float(CAP), ALU.mult, ALU.add))
            L.after(dve.scalar_tensor_tensor(out=j8, in0=ce, scalar=pcol, in1=dl8, op0=ALU.is_le, op1=ALU.mult, accum_out=rc))
            L.after(dve.scalar_tensor_tensor(out=j8, in0=ce, scalar=pcol, in1=ones49[:, 0:EXPERTS], op0=ALU.is_le, op1=ALU.mult, accum_out=ec))
            L.after(dve.scalar_tensor_tensor(out=rc, in0=pcol, scalar=float(P), in1=rc, op0=ALU.mult, op1=ALU.add))
            dve.tensor_scalar(tile_table[:, 0:1], rc, float(PADROW), None, ALU.min)
            dve.tensor_scalar(tile_table[:, 1:2], ec, float(EXPERTS - 1), None, ALU.min).then_inc(s["mtab_ready"], 1)

            L.after(dve.memset(sel[:, :, :], 0.0))
            for e in range(EXPERTS):
                a = dve.tensor_scalar(sel[0:96, e, :], pm[0:96].to_broadcast([96, P]), float(e), None, ALU.is_equal)
            a.then_inc(s["sel_ready"], 1)

            dve.wait_ge(s["moetab_in"], 16)

            dve.wait_ge(s["fold_done"], 2 * EXPERTS)
            dve.wait_ge(s["scattered"], SCATTERED)

            def split_h(i, h):
                dve.wait_ge(pair["gelu"][h], 2 * i + 2)
                split(dve, L, hhi[h], hlo[h], hT[h]).then_inc(pair["h_split"][h], 1)

            def first_layer(i, h):
                e = dve.value_load(moetab[0:1, ds(P + 2 * i + h, 1)], min_val=0, max_val=EXPERTS - 1)
                until(dve, pair["h_mm"][h], 2 * i)
                dve.tensor_copy(w1c[h], w1s[:, ds(e * (DC * HIDDEN), DC * HIDDEN)])
                until(dve, pair["gelu"][h], 2 * i)
                dve.tensor_copy(b1c[h], b1T[:, ds(e * HC, HC)]).then_inc(pair["w1c_ready"][h], 1)
                return e

            def rows(i, h, e):
                dve.wait_ge(pair["xeT_mm"][h], i + 1)
                dve.tensor_copy(wnext[h][:, 0:1], xe[h][:, ds(W_AT + e, 1)])
                L.after(dve.tensor_copy(wnext[h][:, 1:2], xe[h][:, ID_AT:ID_AT + 1]))
                dve.tensor_copy(xeT[h], bank[4 + h][:, 0:D]).then_inc(pair["xeT_ready"][h], 1)

            def weigh(i, h):
                dve.wait_ge(pair["y_mm"][h], i + 1)
                until(dve, pair["y_add"][h], 16 * i)
                dve.tensor_copy(nid[h], wnow[h][:, 1:2])
                dve.tensor_scalar(ys[h], bank[6 + h][:, 0:D], wnow[h][:, 0:1], None, ALU.mult).then_inc(pair["ys_ready"][h], 1)

            def step_on(i, h):
                dve.wait_ge(pair["ys_ready"][h], i + 1)
                L.after(dve.tensor_copy(wnow[h], wnext[h]))
            for h in range(2):
                rows(0, h, first_layer(0, h))
                L.after(dve.tensor_copy(wnow[h], wnext[h]))

            def moe(i, first=False, last=False):
                for h in range(2):
                    if not last:
                        e = first_layer(i + 1, h)
                    split_h(i, h)
                    if h == 1:
                        weigh(i, 0)
                        if not last:
                            step_on(i, 0)
                    elif not first:
                        weigh(i - 1, 1)
                        step_on(i - 1, 1)
                    if not last:
                        rows(i + 1, h, e)
            moe(0, first=True)
            repeat(dve, L, moe, 1, MOE_TILES // 2 - 1)
            moe(MOE_TILES // 2 - 1, last=True)
            weigh(MOE_TILES // 2 - 1, 1)

        @block.tensor
        def _(pe):
            pe.wait_ge(s["consts_dve"], 2)

            def turn_unit(i, h, nt):
                pe.wait_ge(pair["xn_ready"][h], i + 1)
                until(pe, pair["xnT_ready"][h], i)
                for tt in range(nt):
                    for c in range(DC):
                        m = pe.transpose(bank[2 * h + tt // 2][:, (tt % 2) * D + c * P:(tt % 2) * D + (c + 1) * P],
                                         xn[h][:, tt, c * P:(c + 1) * P], ident[:, :])
                m.then_inc(pair["xnT_mm"][h], 1)

            def z_unit(i, h, nt, after_counts=False):
                pe.wait_ge(pair["xnT_ready"][h], i + 1)
                until(pe, pair["z_ready"][h], i)
                if after_counts:
                    pe.wait_ge(s["ecol_ready"], 1)
                for tt in range(nt):
                    for c in range(DC):
                        m = pe.matmul(bank[4 + 2 * h + tt // 2][:, (tt % 2) * D:(tt % 2 + 1) * D], xnT[h][:, tt, c * P:(c + 1) * P],
                                      w_neigh[:, c, :], start=(c == 0), stop=(c == DC - 1))
                m.then_inc(pair["z_mm"][h], 1)

            def ln_iter(i):
                turn_unit(i, 0, 3)
                z_unit(i - 1, 1, 3, after_counts=isinstance(i, int))
                turn_unit(i, 1, 3)
                z_unit(i, 0, 3)
            turn_unit(0, 0, 3)
            turn_unit(0, 1, 3)
            pe.wait_ge(s["neigh_in"], 16)
            z_unit(0, 0, 3)
            pe.wait_ge(s["unsorted_ready"], 1)
            pe.matmul(bank[6][:, 0:1], ones_b[:, :], bad_b[:, 0:1], start=True, stop=True).then_inc(s["unsorted_mm"], 1)
            pe.wait_ge(s["unsorted_ready"], 2)
            with pe.If(pe.value_load(flag[0:1, 0:1], min_val=0, max_val=1) > 0):
                pe.wait_ge(s["bases_mm"], 1)
                pe.matmul(bank[6][:, 0:BUCKETS], ones_f, hot, start=True, stop=True).then_inc(s["bases_mm"], 1)

                def rank_row(row):
                    pe.wait_ge(s["row_hot"], row + 1)
                    pe.matmul(bank[6][:, 0:BUCKETS], before_f, hot, start=True, stop=False)
                    pe.matmul(bank[6][:, 0:BUCKETS], ones_f, seen, start=False, stop=True).then_inc(s["row_rank"], 1)
                repeat(pe, None, rank_row, 0, EROWS)
            pe.wait_ge(s["cmp_ready"], 1)
            for k in range(2):
                for j in range(EJ):
                    m = pe.matmul(bank[6 + k][:, 0:NT], ones_b[0:EP, :], cmpb[0:EP, k * EJ + j, 0:NT], start=(j == 0), stop=(j == EJ - 1))
                m.then_inc(s["counts_ready"], 1)
            repeat(pe, None, ln_iter, 1, UN)
            turn_unit(UN, 0, 1)
            z_unit(UN - 1, 1, 3)
            pe.wait_ge(s["stepsf_ready"], 1)
            pe.wait_ge(pair["xnT_ready"][0], UN + 1)
            pe.wait_ge(pair["xnT_ready"][1], UN)
            for k in range(2):
                for half, (j0, j1) in enumerate(((0, 4), (4, 7))):
                    for j in range(j0, j1):
                        m = pe.transpose(bank[2 * k + half][:, (j - j0) * P:(j - j0 + 1) * P], steps_f[:, j, k, :], ident[:, :])
                    m.then_inc(s["stepT_ready"], 1)
            z_unit(UN, 0, 1)
            pe.wait_ge(pair["z_ready"][0], UN + 1)
            pe.wait_ge(s["tables_ready"], 2)

            def walk(i, hooks={}):
                if -1 in hooks:
                    hooks[-1]()
                for k in range(STEP_BLOCK):
                    step = STEP_BLOCK * i + k
                    pe.wait_ge(g_in[k], 16 * (i + 1))
                    if k % S_GROUP == 0:
                        pe.wait_ge(s["s_built"], 2 * i + k // S_GROUP + 1)
                    if k % 2 == 0:
                        until(pe, s["acc_done"], PAIRS * (i - 1) + k // 2 + 1)
                    pe.matmul(bank[k // 2][:, 0:ACCW], S[:, k // S_GROUP, k % S_GROUP, :], G[:, k, :], start=(k % 2 == 0), stop=(k % 2 == 1)).then_inc(s["p_ready"], 1)
                    if k in hooks:
                        hooks[k]()

            def kv(t):
                pe.wait_ge(s["xa_in"], 16 * (t + 1))
                until(pe, s["kv_act"], t)
                for c in range(DC):
                    m = pe.matmul(bank[4][:, 0:2 * HID], xTs[:, c * P:(c + 1) * P], w_kv[:, c, :], start=(c == 0), stop=(c == DC - 1))
                m.then_inc(s["kv_mm"], 1)
            pe.wait_ge(s["consts_dve"], 4)
            repeat(pe, None, lambda i: walk(i, {6: lambda: kv(i)}), 0, NT - 1)
            kv(NT - 1)
            pe.wait_ge(s["kv_dve"], NT)
            pe.transpose(bank[6][:, 0:P], kmax, ident[:, :]).then_inc(s["kmaxT"], 1)
            pe.wait_ge(s["km_ready"], 1)
            pe.transpose(bank[6][:, 0:P], kmaxb, ident[:, :]).then_inc(s["kmaxrowT"], 1)
            pe.wait_ge(s["mk_exp"], 1)
            pe.matmul(bank[5][:, 0:HID + 2], mkT[:, :], mv1[:, :], start=True, stop=False, skip_group_check=True)

            def ctx_mm(g, nt=8, rows=P, last=False):
                pe.wait_ge(s["ek_exp"], g + 1)
                if isinstance(g, int):
                    pe.wait_ge(s["kv_act"], NT)
                for j in range(nt):
                    m = pe.matmul(bank[5][:, 0:HID + 2], ek[0:rows, j, :],
                                  kv_all[0:rows, ds(8 * g + j, 1), HID:KVW].rearrange("p o w -> p (o w)"),
                                  start=False, stop=last, skip_group_check=True)
                m.then_inc(s["ctx_mm"], 1)
            A2 = NT - 1
            repeat(pe, None, lambda i: walk(i, {7: lambda: ctx_mm(i - A2)}), A2, A2 + 6)
            ctx_mm(6, 1, TAIL, True)
            pe.wait_ge(s["ctx_ready"], 1)
            pe.transpose(bank[6][:, 0:P], ctxs, ident[:, :]).then_inc(s["ctxT_mm"], 1)
            pe.wait_ge(s["ctxT_ready"], 1)
            pe.matmul(bank[7][:, 0:D], ctxT, w_outs, start=True, stop=True).then_inc(s["M2_mm"], 1)
            pe.wait_ge(s["M2_ready"], 1)

            def qu(t):
                pe.wait_ge(s["xb_in"], 16 * (t + 1))
                until(pe, s["qu_evac"], t)
                for c in range(DC):
                    m = pe.matmul(bank[4][:, 0:HID + D], xTs[:, c * P:(c + 1) * P], w_qu[:, c, :], start=(c == 0), stop=(c == DC - 1))
                m.then_inc(s["qu_mm"], 1)

            def turn_q(t):
                pe.wait_ge(s["q_ready"], t + 1)
                pe.transpose(bank[6][:, 0:P], q_s, ident[:, :]).then_inc(s["qT_mm"], 1)

            def mix_out(t):
                pe.wait_ge(s["qT_sb"], t + 1)
                until(pe, s["o_evac"], t)
                pe.matmul(bank[7][:, 0:D], qT_s, M2[:, :], start=True, stop=True).then_inc(s["o_mm"], 1)

            def bfold(e, n):
                until(pe, s["bf_evac"], 2 * e + n)
                for c in range(DC):
                    m = pe.matmul(bank[5][0:EXPERTS, :], lnb[:, c, :], w1s[:, ds((e * DC + c) * HIDDEN + n * 512, 512)],
                                  start=(c == 0), stop=(c == DC - 1))
                m.then_inc(s["bf_mm"], 1)
            B0 = A2 + 6

            def b_hooks(t):
                return {-1: lambda: qu(t), 5: lambda: turn_q(t), 7: lambda: mix_out(t)}

            def fold_hooks(t):
                hk = b_hooks(t)
                e = t - 16
                hk[3] = lambda: bfold(e, 0)
                hk[6] = lambda: bfold(e, 1)
                return hk
            repeat(pe, None, lambda t: walk(t + B0, b_hooks(t)), 0, 16)
            pe.wait_ge(s["w1_in"], 16 * EXPERTS)
            repeat(pe, None, lambda t: walk(t + B0, fold_hooks(t)), 16, 24)
            repeat(pe, None, lambda t: walk(t + B0, b_hooks(t)), 24, NT)
            walk(B0 + NT)
            pe.wait_ge(s["bf_evac"], 2 * EXPERTS)
            for c in range(HC):
                m = pe.matmul(bank[5][:, c * EXPERTS:(c + 1) * EXPERTS], bacc[0:EXPERTS, c * P:(c + 1) * P], ident[0:EXPERTS, 0:EXPERTS],
                              start=True, stop=True)
            m.then_inc(s["b1_mm"], 1)
            repeat(pe, None, walk, B0 + NT + 1, BLOCKS)
            pe.wait_ge(s["acc_done"], PAIRS * BLOCKS)

            def r_turn(it, nt=RT):
                for half in range((nt + 2) // 3):
                    pe.wait_ge(s["h_ready"], 2 * it + half + 1)
                    for tt in range(3 * half, min(3 * half + 3, nt)):
                        at = (tt - 3 * half) % 2 * D
                        for c in range(DC):
                            m = pe.transpose(bank[2 * half + (tt - 3 * half) // 2][:, at + c * P:at + (c + 1) * P],
                                             h6[:, tt, c * P:(c + 1) * P], ident[:, :])
                    m.then_inc(s["hT_mm"], 1)

            def r_logits(it, nt=RT):
                for half in range((nt + 2) // 3):
                    pe.wait_ge(s["hT_ready"], 2 * it + half + 1)
                    for tt in range(3 * half, min(3 * half + 3, nt)):
                        for c in range(DC):
                            m = pe.matmul(bank[6][:, tt * EXPERTS:(tt + 1) * EXPERTS], hT6[:, tt, c * P:(c + 1) * P], Wr_s[:, c, :],
                                          start=(c == 0), stop=(c == DC - 1))
                m.then_inc(s["lg_mm"], 1)

            def r_rank(it, nt=RT):
                pe.wait_ge(s["pick_ready"], it + 1)
                for tt in range(nt):
                    to = bank[5][:, tt * EXPERTS:(tt + 1) * EXPERTS]
                    pe.matmul(to, before[:, :], picked[:, tt, :], start=True, stop=False)
                    for b in range(tt):
                        pe.matmul(to, ones_b[:, :], picked[:, b, :], start=False, stop=False)
                    m = pe.matmul(to, ones_b[:, :], cnt[:, :], start=False, stop=True)
                m.then_inc(s["rank_mm"], 1)

            def route(it):
                r_turn(it)
                r_logits(it)
                r_rank(it)
            repeat(pe, None, route, 0, UN)
            r_turn(UN, 1)
            r_logits(UN, 1)
            r_rank(UN, 1)
            pe.wait_ge(s["pay_ready"], UN + 1)
            pe.matmul(bank[5][:, 64:64 + EXPERTS], ones_b[:, :], cnt[:, :], start=True, stop=True).then_inc(s["mtab_cnt"], 1)

            pe.wait_ge(s["moetab_in"], 16)
            pe.wait_ge(s["sel_ready"], 1)

            def turn_x(i, h):
                pe.wait_ge(pair["xe_in"][h], 16 * (i + 1))
                until(pe, pair["xeT_ready"][h], i)
                for c in range(DC):
                    m = pe.transpose(bank[4 + h][:, c * P:(c + 1) * P], xe[h][:, c * P:(c + 1) * P], ident[:, :])
                m.then_inc(pair["xeT_mm"][h], 1)

            def layer1(i, h):
                pe.wait_ge(pair["w1c_ready"][h], i + 1)
                pe.wait_ge(pair["xeT_ready"][h], i + 1)
                until(pe, pair["gelu"][h], 2 * i)
                for c in range(HC):
                    for k in range(DC):
                        m = pe.matmul(bank[2 * h + c // 4][:, (c % 4) * P:(c % 4 + 1) * P], w1c[h][:, k * HIDDEN + c * P:k * HIDDEN + (c + 1) * P],
                                      xeT[h][:, k * P:(k + 1) * P], start=(k == 0), stop=(k == DC - 1))
                    if c % 4 == 3:
                        m.then_inc(pair["h_mm"][h], 1)

            def layer2(i, h):
                e = pe.value_load(moetab[0:1, ds(P + 2 * i + h, 1)], min_val=0, max_val=EXPERTS - 1)
                to = bank[6 + h][:, 0:D]
                until(pe, pair["ys_ready"][h], i)
                pe.matmul(to, sel[:, ds(e, 1), :].rearrange("p o n -> p (o n)"), brows[:, :], start=True, stop=False)
                pe.wait_ge(pair["h_split"][h], i + 1)
                pe.wait_ge(pair["w2l_in"][h], 16 * (i + 1))
                for c in range(HC):
                    hi, lo = (v[h][:, c * P:(c + 1) * P].bitcast(F32R) for v in (hhi, hlo))
                    w_hi = w2s_r[:, ds(e * (HC * D) + c * D, D)].bitcast(F32R)
                    pe.matmul(to, hi, w_hi, start=False, stop=False)
                    pe.matmul(to, lo, w_hi, start=False, stop=False)
                    m = pe.matmul(to, hi, w2l[h][:, c * D:(c + 1) * D].bitcast(F32R), start=False, stop=(c == HC - 1))
                m.then_inc(pair["y_mm"][h], 1)
            turn_x(0, 0)
            turn_x(0, 1)
            layer1(0, 0)
            pe.wait_ge(s["w2_in"], 16 * EXPERTS)

            def moe(i, last=False):
                layer1(i, 1)
                if not last:
                    turn_x(i + 1, 0)
                layer2(i, 0)
                if not last:
                    layer1(i + 1, 0)
                    turn_x(i + 1, 1)
                layer2(i, 1)
            repeat(pe, None, moe, 0, MOE_TILES // 2 - 1)
            moe(MOE_TILES // 2 - 1, True)


N_WEIGHTS = 20

_INS = ["x", "src", "dst", "L0_gnn_W", "L0_gnn_b", "L0_mix_w_qkv", "L0_mix_mem_kv", "L0_mix_w_out", "L0_mix_b_out",
        "L0_mix_g_out", "L0_mix_g_pre", "L0_ffn_Wr", "L0_ffn_br", "L0_ffn_ln_g", "L0_ffn_ln_b", "L0_ffn_W1",
        "L0_ffn_b1", "L0_ffn_W2", "L0_ffn_b2"]


def kernel(**inputs):
    import numpy as _np
    import concourse.bacc as _bacc
    from concourse import mybir as _mybir
    from concourse.bass_utils import run_bass_kernel_spmd as _run

    nc = _bacc.Bacc("TRN2", target_bir_lowering=False, num_devices=1)
    arrays, args = {}, []
    for name in _INS:
        a = _np.ascontiguousarray(inputs[name])
        arrays[f"in_{name}_dram"] = a
        args.append(nc.dram_tensor(f"in_{name}_dram", a.shape, _mybir.dt.from_np(a.dtype), kind="ExternalInput").ap())
    out = nc.dram_tensor("out_0_dram", (OUT_ROWS, D), F32, kind="ExternalOutput").ap()
    build_program(nc, *args, out)
    r = _run(nc, [arrays], core_ids=[0])
    return r.results[0]["out_0_dram"][0:N]
```
